# Optimizing a Trainium2 kernel written in Bass

```python
import numpy as np
import jax
import jax.numpy as jnp

def _softmax(x, axis=-1):
    return jax.nn.softmax(x, axis=axis)

def _gelu(x):
    return jax.nn.gelu(x, approximate=True)

def _silu(x):
    return jax.nn.silu(x)

def _sigmoid(x):
    return jax.nn.sigmoid(x)

def _layernorm(x, axis=-1, eps=1e-05):
    m = jnp.mean(x, axis=axis, keepdims=True)
    v = jnp.var(x, axis=axis, keepdims=True)
    return (x - m) / jnp.sqrt(v + eps)

def _scatter_add(tgt, idx, src, axis=0):
    return tgt.at[idx].add(src)

def _segment_sum(src, seg, n):
    return jax.ops.segment_sum(src, seg, n)
kernel_name = 'mk_decoder_postln_d1_seqx_r8_941940'

def setup_inputs(seed: int=0):
    np.random.seed(seed)
    _w = jnp.asarray

    def _rec_inputs():
        import jax
        import jax.numpy as jnp
        _rk = jax.random.key(seed)
        x = 7.22e-05 + 1 * jax.random.normal(jax.random.fold_in(_rk, 1), (32, 100, 512), jnp.float32)
        _lenS = 100 - jax.random.randint(jax.random.fold_in(_rk, 7), (32,), 0, max(1, 100 // 4) + 1, jnp.int32)
        _lenS2 = 1444 - jax.random.randint(jax.random.fold_in(_rk, 8), (32,), 0, max(1, 1444 // 4) + 1, jnp.int32)
        _ctx_4096P = jax.random.normal(jax.random.fold_in(_rk, 11), (32, 16, 512), jnp.float32)
        _ctx_4096c = jax.random.dirichlet(jax.random.fold_in(_rk, 511), 0.3 * jnp.ones((16,), jnp.float32), (32, 1444))
        _ctx_4096t = jnp.einsum('bsk,bkd->bsd', _ctx_4096c, _ctx_4096P)
        _ctx_4096t = _ctx_4096t * jax.lax.rsqrt(jnp.mean(jnp.square(_ctx_4096t)) + 1e-12) * 0.953939
        ctx_4096 = 2.81802e-05 + 1.00001 * (_ctx_4096t + 0.3 * jax.random.normal(jax.random.fold_in(_rk, 611), (32, 1444, 512), jnp.float32))
        return (x, ctx_4096)
    x, ctx_4096 = _rec_inputs()

    def _L0_attn_setup():
        import jax, jax.numpy as jnp
        import numpy as np
        HEADS = 32
        key = jax.random.key(seed)
        ks = jax.random.split(key, 5)
        H = 512
        B, S = (2, 256)
        w_scale = 1.0 / np.sqrt(H)
        return {'x': jax.random.normal(ks[0], (B, S, H), dtype=jnp.float32), 'attn_qkvw': jax.random.normal(ks[1], (H, 3 * H), dtype=jnp.float32) * w_scale, 'attn_qkvb': jax.random.normal(ks[2], (3 * H,), dtype=jnp.float32) * 0.02, 'attn_ow': jax.random.normal(ks[3], (H, H), dtype=jnp.float32) * w_scale, 'attn_ob': jax.random.normal(ks[4], (H,), dtype=jnp.float32) * 0.02}
    _L0_attn_all = _L0_attn_setup()
    _L0_attn_in = {k: v for k, v in _L0_attn_all.items() if k in ('attn_qkvw', 'attn_qkvb', 'attn_ow', 'attn_ob')}
    del _L0_attn_all

    def _L0_xattn_setup():
        import jax, jax.numpy as jnp
        import numpy as np
        HIDDEN = 512
        N_HEADS = 32
        N_KV_HEADS = 8
        HEAD_DIM = HIDDEN // N_HEADS
        N_REP = N_HEADS // N_KV_HEADS
        EPS = 1e-05

        def _rmsnorm(x, w):
            xf = x.astype(jnp.float32)
            var = jnp.mean(xf * xf, axis=-1, keepdims=True)
            return (xf * jax.lax.rsqrt(var + EPS)).astype(x.dtype) * w
        key = jax.random.key(seed)
        ks = jax.random.split(key, 7)
        B, Q, K = (2, 128, 256)
        scale = 0.02
        return {'hidden_states': jax.random.normal(ks[0], (B, Q, HIDDEN), jnp.float32), 'encoder_hidden_states': jax.random.normal(ks[1], (B, K, HIDDEN), jnp.float32), 'wq': jax.random.normal(ks[2], (N_HEADS * HEAD_DIM, HIDDEN), jnp.float32) * scale, 'wk': jax.random.normal(ks[3], (N_KV_HEADS * HEAD_DIM, HIDDEN), jnp.float32) * scale, 'wv': jax.random.normal(ks[4], (N_KV_HEADS * HEAD_DIM, HIDDEN), jnp.float32) * scale, 'wo': jax.random.normal(ks[5], (HIDDEN, N_HEADS * HEAD_DIM), jnp.float32) * scale, 'ln_w': jnp.ones((HIDDEN,), jnp.float32)}
    _L0_xattn_all = _L0_xattn_setup()
    _L0_xattn_in = {k: v for k, v in _L0_xattn_all.items() if k in ('wq', 'wk', 'wv', 'wo', 'ln_w')}
    del _L0_xattn_all

    def _L0_ffn_setup():
        import jax, jax.numpy as jnp
        import numpy as np

        def _dequant_linear(x, wq, scale):
            w = wq.astype(jnp.float32) * scale[:, None]
            return jnp.einsum('bsh,oh->bso', x, w)
        key = jax.random.key(seed)
        ks = jax.random.split(key, 7)
        B, S, H, I = (2, 256, 512, 1792)
        x = jax.random.normal(ks[0], (B, S, H), dtype=jnp.float32)
        gate_wq = jax.random.randint(ks[1], (I, H), -128, 128, dtype=jnp.int32)
        up_wq = jax.random.randint(ks[2], (I, H), -128, 128, dtype=jnp.int32)
        down_wq = jax.random.randint(ks[3], (H, I), -128, 128, dtype=jnp.int32)
        gate_scale = jax.random.uniform(ks[4], (I,), dtype=jnp.float32, minval=0.5, maxval=1.5) / (127.0 * np.sqrt(H))
        up_scale = jax.random.uniform(ks[5], (I,), dtype=jnp.float32, minval=0.5, maxval=1.5) / (127.0 * np.sqrt(H))
        down_scale = jax.random.uniform(ks[6], (H,), dtype=jnp.float32, minval=0.5, maxval=1.5) / (127.0 * np.sqrt(I))
        return {'x': x, 'gate_wq': gate_wq, 'gate_scale': gate_scale, 'up_wq': up_wq, 'up_scale': up_scale, 'down_wq': down_wq, 'down_scale': down_scale}
    _L0_ffn_all = _L0_ffn_setup()
    _L0_ffn_in = {k: v for k, v in _L0_ffn_all.items() if k in ('gate_wq', 'gate_scale', 'up_wq', 'up_scale', 'down_wq', 'down_scale')}
    del _L0_ffn_all
    return {'x': x, 'ctx_4096': ctx_4096, 'L0_attn_attn_qkvw': _L0_attn_in['attn_qkvw'], 'L0_attn_attn_qkvb': _L0_attn_in['attn_qkvb'], 'L0_attn_attn_ow': _L0_attn_in['attn_ow'], 'L0_attn_attn_ob': _L0_attn_in['attn_ob'], 'L0_xattn_wq': _L0_xattn_in['wq'], 'L0_xattn_wk': _L0_xattn_in['wk'], 'L0_xattn_wv': _L0_xattn_in['wv'], 'L0_xattn_wo': _L0_xattn_in['wo'], 'L0_xattn_ln_w': _L0_xattn_in['ln_w'], 'L0_ffn_gate_wq': _L0_ffn_in['gate_wq'], 'L0_ffn_gate_scale': _L0_ffn_in['gate_scale'], 'L0_ffn_up_wq': _L0_ffn_in['up_wq'], 'L0_ffn_up_scale': _L0_ffn_in['up_scale'], 'L0_ffn_down_wq': _L0_ffn_in['down_wq'], 'L0_ffn_down_scale': _L0_ffn_in['down_scale']}

def reference(x, ctx_4096, L0_attn_attn_qkvw, L0_attn_attn_qkvb, L0_attn_attn_ow, L0_attn_attn_ob, L0_xattn_wq, L0_xattn_wk, L0_xattn_wv, L0_xattn_wo, L0_xattn_ln_w, L0_ffn_gate_wq, L0_ffn_gate_scale, L0_ffn_up_wq, L0_ffn_up_scale, L0_ffn_down_wq, L0_ffn_down_scale):
    import jax
    import jax.numpy as jnp

    def _L0_attn_ref(x, attn_qkvw, attn_qkvb, attn_ow, attn_ob):
        import jax, jax.numpy as jnp
        import numpy as np
        HEADS = 32
        B, S, H = x.shape
        hd = H // HEADS
        scale = 1.0 / np.sqrt(hd)
        qkv = x @ attn_qkvw + attn_qkvb
        qkv = qkv.reshape(B, S, 3, HEADS, hd)
        q = jnp.transpose(qkv[:, :, 0], (0, 2, 1, 3))
        k = jnp.transpose(qkv[:, :, 1], (0, 2, 1, 3))
        v = jnp.transpose(qkv[:, :, 2], (0, 2, 1, 3))
        scores = jnp.einsum('bhqd,bhkd->bhqk', q, k) * scale
        probs = jax.nn.softmax(scores, axis=-1)
        ctx = jnp.einsum('bhqk,bhkd->bhqd', probs, v)
        ctx = jnp.transpose(ctx, (0, 2, 1, 3)).reshape(B, S, H)
        return ctx @ attn_ow + attn_ob

    def _L0_xattn_ref(hidden_states, encoder_hidden_states, wq, wk, wv, wo, ln_w):
        import jax, jax.numpy as jnp
        import numpy as np
        HIDDEN = 512
        N_HEADS = 32
        N_KV_HEADS = 8
        HEAD_DIM = HIDDEN // N_HEADS
        N_REP = N_HEADS // N_KV_HEADS
        EPS = 1e-05

        def _rmsnorm(x, w):
            xf = x.astype(jnp.float32)
            var = jnp.mean(xf * xf, axis=-1, keepdims=True)
            return (xf * jax.lax.rsqrt(var + EPS)).astype(x.dtype) * w
        B, Qlen, _ = hidden_states.shape
        _, Klen, _ = encoder_hidden_states.shape
        x = _rmsnorm(hidden_states, ln_w)
        q = jnp.einsum('bqd,hd->bqh', x, wq).reshape(B, Qlen, N_HEADS, HEAD_DIM)
        k = jnp.einsum('bkd,hd->bkh', encoder_hidden_states, wk).reshape(B, Klen, N_KV_HEADS, HEAD_DIM)
        v = jnp.einsum('bkd,hd->bkh', encoder_hidden_states, wv).reshape(B, Klen, N_KV_HEADS, HEAD_DIM)
        q = q.transpose(0, 2, 1, 3)
        k = k.transpose(0, 2, 1, 3)
        v = v.transpose(0, 2, 1, 3)
        k = jnp.repeat(k, N_REP, axis=1)
        v = jnp.repeat(v, N_REP, axis=1)
        scores = jnp.einsum('bhqd,bhkd->bhqk', q, k) / np.sqrt(HEAD_DIM).astype(np.float32)
        attn = jax.nn.softmax(scores.astype(jnp.float32), axis=-1).astype(q.dtype)
        out = jnp.einsum('bhqk,bhkd->bhqd', attn, v)
        out = out.transpose(0, 2, 1, 3).reshape(B, Qlen, HIDDEN)
        return jnp.einsum('bqh,dh->bqd', out, wo)

    def _L0_ffn_ref(x, gate_wq, gate_scale, up_wq, up_scale, down_wq, down_scale):
        import jax, jax.numpy as jnp
        import numpy as np

        def _dequant_linear(x, wq, scale):
            w = wq.astype(jnp.float32) * scale[:, None]
            return jnp.einsum('bsh,oh->bso', x, w)
        gate = _dequant_linear(x, gate_wq, gate_scale)
        up = _dequant_linear(x, up_wq, up_scale)
        h = jax.nn.silu(gate) * up
        return _dequant_linear(h, down_wq, down_scale)
    x = _layernorm(x + _L0_attn_ref(x, L0_attn_attn_qkvw, L0_attn_attn_qkvb, L0_attn_attn_ow, L0_attn_attn_ob), axis=-1)
    x = _layernorm(x + _L0_xattn_ref(x, ctx_4096, L0_xattn_wq, L0_xattn_wk, L0_xattn_wv, L0_xattn_wo, L0_xattn_ln_w), axis=-1)
    x = _layernorm(x + _L0_ffn_ref(x, L0_ffn_gate_wq, L0_ffn_gate_scale, L0_ffn_up_wq, L0_ffn_up_scale, L0_ffn_down_wq, L0_ffn_down_scale), axis=-1)
    return x

_drawn_inputs = setup_inputs


def setup_inputs(seed=0):
    import zlib

    import numpy as np

    out = dict(_drawn_inputs(seed))
    spreads = {'L0_xattn_ln_w': (1.0, 0.6)}
    factors = {'L0_attn_attn_qkvb': 2.841,
     'L0_attn_attn_ob': 2.908,
     'L0_xattn_wq': 7.417,
     'L0_xattn_wk': 7.393}
    for name, (base, spread) in spreads.items():
        noise = np.random.default_rng([zlib.crc32(name.encode()), seed]).standard_normal(out[name].shape)
        drawn = base * np.exp(spread * noise) if base else spread * noise
        out[name] = jnp.asarray(drawn.astype(out[name].dtype))
    for name, factor in factors.items():
        out[name] = (out[name] * factor).astype(out[name].dtype)
    return out
```

```python
from contextlib import ExitStack

import concourse.bass as bass
from concourse import mybir

F32 = mybir.dt.float32
F32R = mybir.dt.float32r
BF16 = mybir.dt.bfloat16
I32 = mybir.dt.int32
ALU = mybir.AluOpType
ACT = mybir.ActivationFunctionType
AX = mybir.AxisListType

BATCH, SEQ, HID = 32, 100, 512
CTX = 1444
HEADS, HD = 32, 16
KV = 8
REP = HEADS // KV
FFN = 1792
P = 128
CH = HID // P
EPS = 1e-5
SCALE = 0.25
TERMS = 6
STACK = TERMS * HD
AUG = STACK + 3
VW = 32

KT = 12
KTW = 121
KTN = [min(KTW, CTX - k * KTW) for k in range(KT)]
UW = 482
UNITS = 3
UN = [min(UW, CTX - u * UW) for u in range(UNITS)]


def there(batch):
    return not isinstance(batch, int) or 0 <= batch < BATCH


def run_slots(engine, body, first, steady, after, last):
    for t in range(first, steady):
        body(t // 2, t % 2)
    with engine.Fori(steady // 2, after // 2) as j:
        body(j, 0)
        body(j, 1)
    for t in range(after, last):
        body(t // 2, t % 2)


class Uses:

    def __init__(self, uses, first, steady):
        self.uses, self.first, self.steady = uses, first, steady

    def in_slot(self, t):
        return [name for name, off in self.uses if 0 <= t + off < BATCH]

    def before(self, t, name):
        if isinstance(t, int):
            return sum(len(self.in_slot(s)) for s in range(self.first, t)) + self.in_slot(t).index(name)
        n = len(self.uses)
        at = self.before(self.steady, name) - n * self.steady
        return t * n + at

    def count(self, t, name):
        return self.before(t, name) + 1


def wait_free(engine, read, uses, t, name):
    n = uses.before(t, name)
    if not isinstance(n, int) or n > 0:
        engine.wait_ge(read, n)


def triple(nc, out, lhs, rhs):
    pairs = [(a, b) for a, b in zip(lhs, rhs)]
    last = None
    for n, ((ah, al), (bh, bl)) in enumerate(pairs):
        nc.tensor.matmul(out, ah, bh, start=n == 0, stop=False)
        nc.tensor.matmul(out, ah, bl, start=False, stop=False)
        last = nc.tensor.matmul(out, al, bh, start=False, stop=n == len(pairs) - 1)
    return last


def identity(nc, pool, tile, zeroed):
    nc.gpsimd.memset(tile, 0.0).then_inc(zeroed, 1)
    pool.wait_ge(zeroed, 1)
    return nc.gpsimd.affine_select(out=tile, in_=tile, compare_op=ALU.not_equal, fill=1.0, base=0,
                                   pattern=[[-1, tile.shape[1]]], channel_multiplier=1)


def self_attention(nc, x, xT, wqkv, bqkv, wout, bout, wqT, lnw, x1_out, qstack_out):
    with ExitStack() as ctx:
        def sb(name, shape, dt):
            return ctx.enter_context(nc.sbuf_tensor("a_" + name, shape, dt))

        def sem(name):
            return ctx.enter_context(nc.semaphore("a_" + name))

        wqkv_h = sb("wqkv_h", [P, CH, 3 * HID], F32R)
        wqkv_l = sb("wqkv_l", [P, CH, 3 * HID], F32R)
        wout_h = sb("wout_h", [P, CH, HID], F32R)
        wout_l = sb("wout_l", [P, CH, HID], F32R)
        wq_h = sb("wq_h", [P, CH, HID], F32R)
        wq_l = sb("wq_l", [P, CH, HID], F32R)
        stage = sb("stage", [P, 2, CH * HID], F32)
        bqkv_b = sb("bqkv_b", [SEQ, 3 * HID], F32)
        bout_b = sb("bout_b", [SEQ, HID], F32)
        lnw_b = sb("lnw_b", [SEQ, HID], F32)
        ident = sb("ident", [P, P], F32)
        identb = sb("identb", [P, P], BF16)
        mask = sb("mask", [P, KV], F32)
        half = sb("half", [SEQ, 1], F32)
        eps = sb("eps", [SEQ, 1], F32)
        zero = sb("zero", [P, 1], F32)

        xT_f = sb("xT_f", [P, 2, CH, SEQ], F32)
        xT_h = sb("xT_h", [P, 2, CH, SEQ], F32R)
        xT_l = sb("xT_l", [P, 2, CH, SEQ], F32R)
        xtok = sb("xtok", [SEQ, 2, HID], F32)
        xb = sb("xb", [SEQ, 2, HID], F32)
        qtok = sb("qtok", [SEQ, HID], F32)
        ktok = sb("ktok", [SEQ, HID], F32)
        vaug = sb("vaug", [SEQ, HEADS, VW], F32)
        qT = sb("qT", [P, CH, SEQ], F32)
        kT = sb("kT", [P, CH, SEQ], F32)
        kdiag = sb("kdiag", [P, CH, KV, SEQ], F32)
        smax = sb("smax", [SEQ, CH, KV], F32)
        prob = sb("prob", [SEQ, CH, KV, SEQ], F32)
        pT = sb("pT", [SEQ, 2, 4, SEQ], F32)
        oT = sb("oT", [P, KV, SEQ], F32)
        rsum = sb("rsum", [SEQ, HEADS], F32)
        otok = sb("otok", [SEQ, HID], F32)
        oT_h = sb("oT_h", [P, CH, SEQ], F32R)
        oT_l = sb("oT_l", [P, CH, SEQ], F32R)
        res = sb("res", [SEQ, HID], F32)
        stats = sb("stats", [SEQ, 6], F32)
        mv = sb("mv", [SEQ, 2], F32)
        ve = sb("ve", [SEQ, 1], F32)
        rstd = sb("rstd", [SEQ, 1], F32)
        x1 = sb("x1", [SEQ, 2, HID], F32)
        junk = sb("junk", [SEQ, HID], F32)
        ssq = sb("ssq", [SEQ, 1], F32)
        me = sb("me", [SEQ, 1], F32)
        rrms = sb("rrms", [SEQ, 1], F32)
        hn = sb("hn", [SEQ, HID], F32)
        hT_h = sb("hT_h", [P, CH, SEQ], F32R)
        hT_l = sb("hT_l", [P, CH, SEQ], F32R)
        qf = sb("qf", [SEQ, HEADS, HD], F32)
        qr = sb("qr", [SEQ, HEADS, HD], F32)
        qparts = sb("qparts", [SEQ, HEADS, P], BF16)
        qstk = sb("qstk", [STACK, 2, 16 * SEQ], BF16)

        ps_s = ctx.enter_context(nc.psum_tensor("a_ps_s", [P, 4, 512], F32))
        ps_x = ctx.enter_context(nc.psum_tensor("a_ps_x", [P, 4, 512], F32))

        w_in = [sem(f"w_in{i}") for i in range(2)]
        w_high = sem("w_high")
        w_split = sem("w_split")
        const_in = sem("const_in")
        zeroed = sem("zeroed")
        const_done = sem("const_done")
        xT_in = [sem(f"xT_in{i}") for i in range(2)]
        xtok_in = [sem(f"xtok_in{i}") for i in range(2)]
        x1_sent = [sem(f"x1_sent{i}") for i in range(2)]
        stk_sent = sem("stk_sent")
        xT_high = sem("xT_high")
        xsplit = sem("xsplit")
        xb_done = sem("xb_done")
        kdiag_dve = sem("kdiag_dve")
        kdiag_pool = sem("kdiag_pool")
        max_done = sem("max_done")
        exp_done = sem("exp_done")
        rsum_done = sem("rsum_done")
        oT_high = sem("oT_high")
        stats_done = sem("stats_done")
        mv_done = sem("mv_done")
        ve_done = sem("ve_done")
        rstd_done = sem("rstd_done")
        x1_done = sem("x1_done")
        ssq_done = sem("ssq_done")
        me_done = sem("me_done")
        rrms_done = sem("rrms_done")
        hn_done = sem("hn_done")
        hT_high = sem("hT_high")
        qhi_done = sem("qhi_done")
        qr_done = sem("qr_done")
        qmid_done = sem("qmid_done")
        qlo_done = sem("qlo_done")

        steady, after, last = 2, BATCH, BATCH + 2
        pair = [Uses([("SK0", -2), ("S0", 0), ("S2", 0), ("HT", -1)], 0, steady),
                Uses([("SK1", -2), ("S1", 0), ("S3", 0), ("QP", -1)], 0, steady)]
        bank = [Uses([("OT1", -1), ("QT", 0), ("OP", -1), ("PT1", 0), ("PT3", 0), ("PT5", 0), ("PT7", 0)], 0, steady),
                Uses([("K", 0), ("KT", 0), ("PV0", 0)], 0, steady),
                Uses([("Q", 0), ("V", 0), ("PV1", 0)], 0, steady),
                Uses([("OT0", -1), ("OTT", -1), ("PT0", 0), ("PT2", 0), ("PT4", 0), ("PT6", 0)], 0, steady)]
        s_full = [sem(f"s_full{i}") for i in range(2)]
        s_read = [sem(f"s_read{i}") for i in range(2)]
        x_full = [sem(f"x_full{i}") for i in range(4)]
        x_read = [sem(f"x_read{i}") for i in range(4)]

        def tokens4(ps, i):
            return ps[:, i, 0:4 * SEQ].rearrange("p (c q) -> p c q", c=4)

        pieces = [(wqkv[:, n * HID:(n + 1) * HID], wqkv_h[:, :, n * HID:(n + 1) * HID],
                   wqkv_l[:, :, n * HID:(n + 1) * HID]) for n in (1, 0, 2)]
        pieces += [(wout, wout_h[:, :, :], wout_l[:, :, :]), (wqT, wq_h[:, :, :], wq_l[:, :, :])]

        block = ctx.enter_context(nc.Block())

        @block.sync
        def _(sp):
            sp.dma_start(bqkv_b[:, :], bqkv.partition_broadcast(SEQ)).then_inc(const_in, 16)
            sp.dma_start(bout_b[:, :], bout.partition_broadcast(SEQ)).then_inc(const_in, 16)
            sp.dma_start(lnw_b[:, :], lnw.partition_broadcast(SEQ)).then_inc(const_in, 16)
            for t in range(2):
                sp.dma_start(xT_f[:, t], xT[t].rearrange("(c p) q -> p c q", p=P)).then_inc(xT_in[t], 16)
                sp.dma_start(xtok[:, t, :], x[t]).then_inc(xtok_in[t], 16)
            for n, (src, _high, _low) in enumerate(pieces):
                if n >= 2:
                    sp.wait_ge(w_split, n - 1)
                sp.dma_start(stage[:, n % 2, :].rearrange("p (c n) -> p c n", c=CH),
                             src.rearrange("(c p) n -> p c n", p=P)).then_inc(w_in[n % 2], 16)

            def body(j, p, ahead):
                t = j * 2 + p
                f, k = there(t), there(t - 1)
                if f and ahead:
                    sp.wait_ge(xsplit, t + 1)
                    sp.dma_start(xT_f[:, p], xT[t + 2].rearrange("(c p) q -> p c q", p=P)).then_inc(xT_in[p], 16)
                    sp.wait_ge(xb_done, t + 1)
                    sp.dma_start(xtok[:, p, :], x[t + 2]).then_inc(xtok_in[p], 16)
                if there(t - 2):
                    sp.wait_ge(s_read[0], pair[0].count(t, "SK0"))
                    sp.wait_ge(s_read[1], pair[1].count(t, "SK1"))
                    sp.dma_start(qstack_out[t - 2], qstk[:, :, :].rearrange("p a n -> p (a n)")).then_inc(stk_sent, 16)
                if k:
                    sp.wait_ge(x1_done, t)
                    sp.dma_start(x1_out[t - 1], x1[:, 1 - p, :]).then_inc(x1_sent[1 - p], 16)

            body(0, 0, True)
            body(0, 1, True)
            with sp.Fori(1, BATCH // 2 - 1) as j:
                body(j, 0, True)
                body(j, 1, True)
            for t in range(BATCH - 2, last):
                body(t // 2, t % 2, False)
            for i in range(2):
                sp.wait_ge(x1_sent[i], 16 * (BATCH // 2))
            sp.wait_ge(stk_sent, 16 * BATCH)

        @block.tensor
        def _(pe):
            pe.wait_ge(const_done, 8)

            def weights(t, piece):
                if isinstance(t, int) and t == (0 if piece < 3 else 1):
                    pe.wait_ge(w_split, piece + 1)

            def use(i, t, name):
                wait_free(pe, x_read[i], bank[i], t, name)

            def project(out, left, wh, wl, col):
                return triple(nc, out, left, [(wh[:, c, col:col + HID], wl[:, c, col:col + HID]) for c in range(CH)])

            def turn_rows(ps, i, src):
                for c in range(CH):
                    done = nc.tensor.transpose(ps[:, i, c * SEQ:(c + 1) * SEQ], src[:, c * P:(c + 1) * P],
                                               ident[0:SEQ, 0:SEQ])
                return done

            def scores(t, u):
                i = u % 2
                wait_free(pe, s_read[i], pair[i], t, f"S{u}")
                pe.wait_ge(kdiag_pool if u % 2 else kdiag_dve, t * 2 + u // 2 + 1)
                for n in range(2):
                    done = nc.tensor.matmul(ps_s[0:SEQ, 2 * i + n, 0:4 * SEQ], qT[:, u, :],
                                            kdiag[:, u, 4 * n:4 * n + 4, :], start=True, stop=True)
                done.then_inc(s_full[i], 1)

            def turn_probs(t, g):
                i = 3 if g % 2 == 0 else 0
                pe.wait_ge(exp_done, t * CH + g // 2 + 1)
                use(i, t, f"PT{g}")
                for c in range(4):
                    done = nc.tensor.transpose(ps_x[0:SEQ, i, c * SEQ:(c + 1) * SEQ],
                                               prob[:, g // 2, 4 * (g % 2) + c, :], ident[0:SEQ, 0:SEQ])
                done.then_inc(x_full[i], 1)

            def values(t, g):
                i = 1 + g // 4
                if g % 4 == 0:
                    use(i, t, f"PV{g // 4}")
                turned = 3 if g % 2 == 0 else 0
                pe.wait_ge(x_read[turned], bank[turned].count(t, f"PT{g}"))
                for c in range(4):
                    done = nc.tensor.matmul(ps_x[VW * c:VW * (c + 1), i, (g % 4) * SEQ:(g % 4 + 1) * SEQ],
                                            vaug[:, 4 * g + c, :], pT[:, g % 2, c, :], start=True, stop=True)
                if g % 4 == 3:
                    done.then_inc(x_full[i], 1)

            def stack(t, n):
                wait_free(pe, s_read[n], pair[n], t, f"SK{n}")
                for h in range(16):
                    out = ps_s[0:P, 2 * n + h // 8, :].bitcast(BF16)[:, (h % 8) * SEQ:(h % 8 + 1) * SEQ]
                    done = nc.tensor.transpose(out, qparts[:, 16 * n + h, :], identb[0:SEQ, 0:SEQ])
                done.then_inc(s_full[n], 1)

            def body(j, p):
                t = j * 2 + p
                f, k = there(t), there(t - 1)
                left = [(xT_h[:, p, c, :], xT_l[:, p, c, :]) for c in range(CH)]
                if f:
                    pe.wait_ge(xsplit, t + 1)
                    weights(t, 0)
                    use(1, t, "K")
                    project(ps_x[0:SEQ, 1, :], left, wqkv_h, wqkv_l, HID).then_inc(x_full[1], 1)
                if k:
                    for n, i in ((0, 3), (1, 0)):
                        pe.wait_ge(x_read[1 + n], bank[1 + n].count(t - 1, f"PV{n}"))
                        use(i, t, f"OT{n}")
                        for g in range(4):
                            done = nc.tensor.transpose(ps_x[0:SEQ, i, g * P:(g + 1) * P], oT[:, 4 * n + g, :], ident[:, :])
                        done.then_inc(x_full[i], 1)
                if f:
                    weights(t, 1)
                    use(2, t, "Q")
                    project(ps_x[0:SEQ, 2, :], left, wqkv_h, wqkv_l, 0).then_inc(x_full[2], 1)
                    use(1, t, "KT")
                    turn_rows(ps_x, 1, ktok).then_inc(x_full[1], 1)
                if k:
                    pe.wait_ge(x_read[0], bank[0].count(t, "OT1"))
                    use(3, t, "OTT")
                    turn_rows(ps_x, 3, otok).then_inc(x_full[3], 1)
                if there(t - 2):
                    pe.wait_ge(qlo_done, t - 1)
                    stack(t, 0)
                    stack(t, 1)
                if f:
                    pe.wait_ge(x_read[2], bank[2].count(t, "Q"))
                    use(0, t, "QT")
                    turn_rows(ps_x, 0, qtok).then_inc(x_full[0], 1)
                    weights(t, 2)
                    use(2, t, "V")
                    project(ps_x[0:SEQ, 2, :], left, wqkv_h, wqkv_l, 2 * HID).then_inc(x_full[2], 1)
                    pe.wait_ge(x_read[0], bank[0].count(t, "QT"))
                    scores(t, 0)
                    scores(t, 1)
                if k:
                    weights(t, 3)
                    pe.wait_ge(x_read[3], bank[3].count(t, "OTT"))
                    use(0, t, "OP")
                    project(ps_x[0:SEQ, 0, :], [(oT_h[:, c, :], oT_l[:, c, :]) for c in range(CH)], wout_h, wout_l,
                            0).then_inc(x_full[0], 1)
                if f:
                    scores(t, 2)
                    scores(t, 3)
                    pe.wait_ge(x_read[2], bank[2].count(t, "V"))
                    for g in range(7):
                        turn_probs(t, g)
                        if g > 0:
                            values(t, g - 1)
                if k:
                    pe.wait_ge(hn_done, t)
                    wait_free(pe, s_read[0], pair[0], t, "HT")
                    turn_rows(ps_s, 0, hn).then_inc(s_full[0], 1)
                if f:
                    turn_probs(t, 7)
                    values(t, 6)
                    values(t, 7)
                if k:
                    weights(t, 4)
                    pe.wait_ge(s_read[0], pair[0].count(t, "HT"))
                    wait_free(pe, s_read[1], pair[1], t, "QP")
                    project(ps_s[0:SEQ, 2, :], [(hT_h[:, c, :], hT_l[:, c, :]) for c in range(CH)], wq_h, wq_l,
                            0).then_inc(s_full[1], 1)

            run_slots(pe, body, 0, steady, after, last)

        @block.scalar
        def _(act):
            def convert(n):
                act.wait_ge(w_in[n % 2], 16 * (n // 2 + 1))
                nc.scalar.copy(pieces[n][1], stage[:, n % 2, :].rearrange("p (c n) -> p c n", c=CH)).then_inc(w_high, 1)

            for n in range(3):
                convert(n)
            act.wait_ge(const_done, 8)

            def body(j, p):
                t = j * 2 + p
                f, k = there(t), there(t - 1)

                def exp(u):
                    act.wait_ge(s_read[u % 2], pair[u % 2].count(t, f"S{u}"))
                    nc.scalar.activation(prob[:, u], prob[:, u], ACT.Exp).then_inc(exp_done, 1)

                def turned(g):
                    i = 3 if g % 2 == 0 else 0
                    act.wait_ge(x_full[i], bank[i].count(t, f"PT{g}"))
                    nc.scalar.copy(pT[:, g % 2], ps_x[0:SEQ, i, 0:4 * SEQ].rearrange("p (c q) -> p c q", c=4)
                                   ).then_inc(x_read[i], 1)

                def outputs(n):
                    act.wait_ge(x_full[1 + n], bank[1 + n].count(t, f"PV{n}"))
                    nc.scalar.copy(oT[:, 4 * n:4 * n + 4, :], tokens4(ps_x, 1 + n)).then_inc(x_read[1 + n], 1)

                if f:
                    act.wait_ge(x_full[1], bank[1].count(t, "KT"))
                    nc.scalar.copy(kT[:, :, :], tokens4(ps_x, 1)).then_inc(x_read[1], 1)
                if there(t - 2):
                    if not isinstance(t, int) or t > 2:
                        act.wait_ge(stk_sent, (t - 2) * 16)
                    for n in range(2):
                        act.wait_ge(s_full[n], pair[n].count(t, f"SK{n}"))
                        nc.scalar.copy(qstk[:, n, :].rearrange("p (a m) -> p a m", a=2),
                                       ps_s[0:STACK, 2 * n:2 * n + 2, :].bitcast(BF16)[:, :, 0:8 * SEQ]).then_inc(s_read[n], 1)
                if f:
                    act.wait_ge(x_full[0], bank[0].count(t, "QT"))
                    nc.scalar.mul(qT[:, :, :], tokens4(ps_x, 0), SCALE).then_inc(x_read[0], 1)
                    exp(0)
                    exp(1)
                    turned(0)
                    exp(2)
                    turned(1)
                    turned(2)
                if k:
                    act.wait_ge(x1_done, t)
                    nc.scalar.activation(junk[:, :], x1[:, 1 - p, :], ACT.Square, scale=HID ** -0.5,
                                         accum_out=ssq[:, :]).then_inc(ssq_done, 1)
                if f:
                    turned(3)
                    exp(3)
                    turned(5)
                    turned(6)
                    turned(7)
                    outputs(1)
                if isinstance(t, int) and t == 0:
                    convert(3)
                    convert(4)

            run_slots(act, body, 0, steady, after, last)

        @block.vector
        def _(dve):
            def convert(n):
                st = stage[:, n % 2, :].rearrange("p (c n) -> p c n", c=CH)
                dve.wait_ge(w_high, n + 1)
                nc.vector.tensor_tensor(pieces[n][2], st, pieces[n][1].bitcast(F32), ALU.subtract).then_inc(w_split, 1)

            for n in range(3):
                convert(n)
            dve.wait_ge(const_done, 8)
            dve.wait_ge(const_in, 48)

            def split(src, full, read, n, high, low, high_done, t):
                dve.wait_ge(full, n)
                nc.vector.tensor_copy(high[:, :, :], src).then_inc(high_done, 1)
                dve.wait_ge(high_done, t)
                nc.vector.tensor_tensor(low[:, :, :], src, high[:, :, :].bitcast(F32), ALU.subtract).then_inc(read, 1)

            def keys_diag(u):
                return nc.vector.tensor_tensor(kdiag[:, u], kT[:, u, :].unsqueeze(1).to_broadcast([P, KV, SEQ]),
                                               mask[:, :].unsqueeze(2).to_broadcast([P, KV, SEQ]), ALU.mult)

            def softmax_sub(t, u):
                i = u % 2
                s = ps_s[0:SEQ, 2 * i:2 * i + 2, 0:4 * SEQ].rearrange("p a (h k) -> p a h k", h=4)
                m = smax[:, u, :].rearrange("p (a h) -> p a h", a=2)
                dve.wait_ge(s_full[i], pair[i].count(t, f"S{u}"))
                nc.vector.tensor_reduce(m, s, AX.X, ALU.max).then_inc(max_done, 1)
                dve.wait_ge(max_done, t * CH + u + 1)
                nc.vector.tensor_tensor(prob[:, u].rearrange("p (a h) k -> p a h k", a=2), s,
                                        m.unsqueeze(3).to_broadcast([SEQ, 2, 4, SEQ]), ALU.subtract).then_inc(s_read[i], 1)

            def body(j, p):
                t = j * 2 + p
                f, k = there(t), there(t - 1)

                def turned(g):
                    i = 3 if g % 2 == 0 else 0
                    dve.wait_ge(x_full[i], bank[i].count(t, f"PT{g}"))
                    nc.vector.tensor_copy(pT[:, g % 2], ps_x[0:SEQ, i, 0:4 * SEQ].rearrange("p (c q) -> p c q", c=4)
                                          ).then_inc(x_read[i], 1)

                def outputs(n):
                    dve.wait_ge(x_full[1 + n], bank[1 + n].count(t, f"PV{n}"))
                    nc.vector.tensor_copy(oT[:, 4 * n:4 * n + 4, :], tokens4(ps_x, 1 + n)).then_inc(x_read[1 + n], 1)

                def biased(i, name, dst, col):
                    dve.wait_ge(x_full[i], bank[i].count(t, name))
                    nc.vector.tensor_tensor(dst[:, :], ps_x[0:SEQ, i, :], bqkv_b[:, col:col + HID], ALU.add
                                            ).then_inc(x_read[i], 1)

                if f:
                    biased(1, "K", ktok, HID)
                if k:
                    for n, i in ((0, 3), (1, 0)):
                        o = ps_x[0:SEQ, i, :].rearrange("p (h v) -> p h v", v=VW)
                        dve.wait_ge(x_full[i], bank[i].count(t, f"OT{n}"))
                        nc.vector.reciprocal(rsum[:, 16 * n:16 * n + 16], o[:, :, HD]).then_inc(rsum_done, 1)
                        dve.wait_ge(rsum_done, t * 2 - 1 + n)
                        nc.vector.tensor_tensor(otok[:, n * 256:(n + 1) * 256].rearrange("p (h d) -> p h d", d=HD),
                                                o[:, :, 0:HD], rsum[:, 16 * n:16 * n + 16].unsqueeze(2).to_broadcast([SEQ, 16, HD]),
                                                ALU.mult).then_inc(x_read[i], 1)
                if f:
                    biased(2, "Q", qtok, 0)
                if k:
                    split(tokens4(ps_x, 3), x_full[3], x_read[3], bank[3].count(t, "OTT"), oT_h, oT_l, oT_high, t)
                if f:
                    dve.wait_ge(x_read[1], bank[1].count(t, "KT"))
                    keys_diag(0).then_inc(kdiag_dve, 1)
                    keys_diag(2).then_inc(kdiag_dve, 1)
                    dve.wait_ge(x_full[2], bank[2].count(t, "V"))
                    nc.vector.tensor_tensor(vaug[:, :, 0:HD], ps_x[0:SEQ, 2, :].rearrange("p (h d) -> p h d", h=HEADS),
                                            bqkv_b[:, 2 * HID:3 * HID].rearrange("p (h d) -> p h d", h=HEADS),
                                            ALU.add).then_inc(x_read[2], 1)
                    softmax_sub(t, 0)
                    softmax_sub(t, 1)
                if k:
                    dve.wait_ge(x_full[0], bank[0].count(t, "OP"))
                    dve.wait_ge(xb_done, t)
                    nc.vector.tensor_tensor(res[:, :], ps_x[0:SEQ, 0, :], xb[:, 1 - p, :], ALU.add).then_inc(x_read[0], 1)
                    dve.wait_ge(x_read[0], bank[0].count(t, "OP"))
                    nc.vector.bn_stats(stats[:, :], res[:, :]).then_inc(stats_done, 1)
                    dve.wait_ge(const_done, 8)
                    dve.wait_ge(stats_done, t)
                    nc.vector.bn_aggr(mv[:, :], stats[:, :]).then_inc(mv_done, 1)
                if f:
                    softmax_sub(t, 2)
                if k:
                    dve.wait_ge(rstd_done, t)
                    b = j + (p - 1) // 2
                    if not isinstance(b, int) or b > 0:
                        dve.wait_ge(x1_sent[1 - p], b * 16)
                    nc.vector.tensor_scalar(x1[:, 1 - p, :], res[:, :], mv[:, 0:1], rstd[:, :], ALU.subtract,
                                            ALU.mult).then_inc(x1_done, 1)
                if f:
                    softmax_sub(t, 3)
                    turned(4)
                    outputs(0)
                if isinstance(t, int) and t == 0:
                    convert(3)
                    convert(4)
                if k:
                    dve.wait_ge(rrms_done, t)
                    nc.vector.scalar_tensor_tensor(hn[:, :], x1[:, 1 - p, :], rrms[:, :], lnw_b[:, :], ALU.mult,
                                                   ALU.mult).then_inc(hn_done, 1)
                    split(tokens4(ps_s, 0), s_full[0], s_read[0], pair[0].count(t, "HT"), hT_h, hT_l, hT_high, t)
                    hi = qparts[:, :, 0:HD]
                    mid = qparts[:, :, 3 * HD:4 * HD]
                    dve.wait_ge(s_full[1], pair[1].count(t, "QP"))
                    nc.vector.tensor_scalar(qf[:, :, :], ps_s[0:SEQ, 2, :].rearrange("p (h d) -> p h d", h=HEADS), SCALE,
                                            None, ALU.mult).then_inc(s_read[1], 1)
                    dve.wait_ge(s_read[1], pair[1].count(t, "QP"))
                    nc.vector.tensor_copy(qparts[:, :, 0:3 * HD].rearrange("p h (r d) -> p h r d", r=3),
                                          qf[:, :, :].unsqueeze(2).to_broadcast([SEQ, HEADS, 3, HD])).then_inc(qhi_done, 1)
                    dve.wait_ge(qhi_done, t)
                    nc.vector.tensor_tensor(qr[:, :, :], qf[:, :, :], hi, ALU.subtract).then_inc(qr_done, 1)
                    dve.wait_ge(qr_done, t)
                    nc.vector.tensor_copy(qparts[:, :, 3 * HD:5 * HD].rearrange("p h (r d) -> p h r d", r=2),
                                          qr[:, :, :].unsqueeze(2).to_broadcast([SEQ, HEADS, 2, HD])).then_inc(qmid_done, 1)
                    dve.wait_ge(qmid_done, t)
                    nc.vector.tensor_tensor(qparts[:, :, 5 * HD:6 * HD], qr[:, :, :], mid, ALU.subtract).then_inc(qlo_done, 1)

            run_slots(dve, body, 0, steady, after, last)

        @block.gpsimd
        def _(pool):
            identity(nc, pool, ident[:, :], zeroed).then_inc(const_done, 1)
            nc.gpsimd.memset(identb[:, :], 0.0).then_inc(zeroed, 1)
            nc.gpsimd.memset(mask[:, :], 1.0).then_inc(zeroed, 1)
            nc.gpsimd.memset(vaug[:, :, :], 0.0).then_inc(zeroed, 1)
            pool.wait_ge(zeroed, 4)
            nc.gpsimd.affine_select(out=identb[:, :], in_=identb[:, :], compare_op=ALU.not_equal, fill=1.0, base=0,
                                    pattern=[[-1, P]], channel_multiplier=1).then_inc(const_done, 1)
            nc.gpsimd.affine_select(out=mask[:, :], in_=mask[:, :], compare_op=ALU.is_ge, fill=0.0, base=0,
                                    pattern=[[-HD, KV]], channel_multiplier=1).then_inc(zeroed, 1)
            pool.wait_ge(zeroed, 5)
            nc.gpsimd.affine_select(out=mask[:, :], in_=mask[:, :], compare_op=ALU.is_ge, fill=0.0, base=HD - 1,
                                    pattern=[[HD, KV]], channel_multiplier=-1).then_inc(const_done, 1)
            nc.gpsimd.memset(vaug[:, :, HD:HD + 1], 1.0).then_inc(const_done, 1)
            nc.gpsimd.memset(half[:, :], -0.5).then_inc(const_done, 1)
            nc.gpsimd.memset(eps[:, :], EPS).then_inc(const_done, 1)
            nc.gpsimd.memset(zero[:, :], 0.0).then_inc(const_done, 1)
            nc.gpsimd.memset(qparts[:, :, STACK:P], 0.0).then_inc(const_done, 1)
            pool.wait_ge(const_done, 8)
            pool.wait_ge(const_in, 48)

            def split_x(t, q, loaded):
                pool.wait_ge(xT_in[q], loaded * 16)
                nc.gpsimd.tensor_tensor(xT_h[:, q], xT_f[:, q], zero[:, :].unsqueeze(2).to_broadcast([P, CH, SEQ]), ALU.add).then_inc(xT_high, 1)
                pool.wait_ge(xT_high, t + 1)
                nc.gpsimd.tensor_tensor(xT_l[:, q], xT_f[:, q], xT_h[:, q].bitcast(F32), ALU.subtract).then_inc(xsplit, 1)

            def body(j, p, ahead):
                t = j * 2 + p
                f, k = there(t), there(t - 1)
                if f:
                    if not isinstance(t, int) or t >= 2:
                        pool.wait_ge(x_read[0], bank[0].count(t - 1, "OP"))
                    pool.wait_ge(xtok_in[p], (j + 1) * 16)
                    nc.gpsimd.tensor_tensor(xb[:, p, :], xtok[:, p, :], bout_b[:, :], ALU.add).then_inc(xb_done, 1)
                    pool.wait_ge(x_read[1], bank[1].count(t, "KT"))
                    for u in (1, 3):
                        nc.gpsimd.tensor_tensor(kdiag[:, u], kT[:, u, :].unsqueeze(1).to_broadcast([P, KV, SEQ]),
                                                mask[:, :].unsqueeze(2).to_broadcast([P, KV, SEQ]), ALU.mult
                                                ).then_inc(kdiag_pool, 1)
                if k:
                    pool.wait_ge(mv_done, t)
                    nc.gpsimd.tensor_tensor(ve[:, :], mv[:, 1:2], eps[:, :], ALU.add).then_inc(ve_done, 1)
                    pool.wait_ge(ve_done, t)
                    nc.gpsimd.tensor_tensor(rstd[:, :], ve[:, :], half[:, :], ALU.pow).then_inc(rstd_done, 1)
                    pool.wait_ge(ssq_done, t)
                    nc.gpsimd.tensor_tensor(me[:, :], ssq[:, :], eps[:, :], ALU.add).then_inc(me_done, 1)
                    pool.wait_ge(me_done, t)
                    nc.gpsimd.tensor_tensor(rrms[:, :], me[:, :], half[:, :], ALU.pow).then_inc(rrms_done, 1)
                if ahead:
                    if not isinstance(t, int) or t >= 1:
                        pool.wait_ge(x_full[2], bank[2].count(t - 1, "V"))
                    split_x(t + 1, 1 - p, j + 1 + p)

            split_x(0, 0, 1)
            body(0, 0, True)
            body(0, 1, True)
            with pool.Fori(1, BATCH // 2 - 1) as j:
                body(j, 0, True)
                body(j, 1, True)
            for t in range(BATCH - 2, last):
                body(t // 2, t % 2, t < BATCH - 1)


def cross_attention(nc, ctxT, wkT, wvT, qstack, kparts, o_out):
    with ExitStack() as ctx:
        def sb(name, shape, dt):
            return ctx.enter_context(nc.sbuf_tensor("c_" + name, shape, dt))

        def sem(name):
            return ctx.enter_context(nc.semaphore("c_" + name))

        STEPS = 2 * KT
        MU = HEADS * UNITS
        PER = MU // STEPS
        LEAD = 6
        HH = HEADS // 2

        wk = sb("wk", [P, CH, P], F32)
        wk_h = sb("wk_h", [P, CH, P], F32R)
        wk_l = sb("wk_l", [P, CH, P], F32R)
        cx_h = sb("cx_h", [P, CH, UW], F32R)
        cx_l = sb("cx_l", [P, CH, UW], F32R)
        wv = sb("wv", [P, CH, P], F32)
        ident = sb("ident", [P, P], F32)
        identb = sb("identb", [P, P], BF16)
        ctx_sb = sb("ctx", [P, 2, CH, CTX], F32)
        kst = sb("kst", [P, 2, KV, CTX], BF16)
        qst = sb("qst", [P, 2, HEADS, SEQ], BF16)
        vaug = sb("vaug", [KTW, 2, KT, KV, VW], F32)
        prob = sb("prob", [KTW, 2, 4, 4 * SEQ], F32)
        kp = sb("kp", [P, 2, 3, UW], BF16)
        kr = sb("kr", [P, 2, UW], F32)
        pmax = sb("pmax", [SEQ, HEADS, UNITS], F32)
        zero = sb("zero", [P, 1], F32)
        nmax = sb("nmax", [SEQ, HH], F32)
        nrest = sb("nrest", [SEQ, HH], F32)
        mparts = sb("mparts", [SEQ, P], BF16)
        mpart = [mparts[:, r * HH:(r + 1) * HH] for r in range(3)]
        mrow = sb("mrow", [3 * HH, SEQ], BF16)
        oT = sb("oT", [P, 4 * SEQ], F32)
        rsum = sb("rsum", [SEQ, HH], F32)
        otok = sb("otok", [SEQ, HID], F32)

        ps_st = ctx.enter_context(nc.psum_tensor("c_ps_st", [P, 4, 512], F32))
        ps_mx = ctx.enter_context(nc.psum_tensor("c_ps_mx", [P, 2, 512], F32))
        ps_pv = ctx.enter_context(nc.psum_tensor("c_ps_pv", [P, 512], F32))
        ps_w = ctx.enter_context(nc.psum_tensor("c_ps_w", [P, 512], F32))

        w_in = sem("w_in")
        wv_in = sem("wv_in")
        zeroed = sem("zeroed")
        const_done = sem("const_done")
        ctx_in = [sem(f"ctx_in{i}") for i in range(2)]
        ctx_first = [sem(f"ctx_first{u}") for u in range(UNITS - 1)]
        kst_in = [sem(f"kst_in{i}") for i in range(2)]
        qst_in = [sem(f"qst_in{i}") for i in range(2)]
        kp_sent = [sem(f"kp_sent{i}") for i in range(2)]
        mrow_in = sem("mrow_in")
        o_sent = [sem(f"o_sent{i}") for i in range(2)]
        st_full = sem("st_full")
        exp_done = sem("exp_done")
        pv_done = sem("pv_done")
        pv_read = sem("pv_read")
        mx_full = sem("mx_full")
        mx_read = sem("mx_read")
        w_full = sem("w_full")
        w_read = sem("w_read")
        wk_high = sem("wk_high")
        wk_split = sem("wk_split")
        cx_high = sem("cx_high")
        cx_split = sem("cx_split")
        cx_used = sem("cx_used")
        khi_done = sem("khi_done")
        kmid_done = sem("kmid_done")
        klo_done = sem("klo_done")
        nmax_done = sem("nmax_done")
        mhi_done = sem("mhi_done")
        nrest_done = sem("nrest_done")
        mmid_done = sem("mmid_done")
        mlo_done = sem("mlo_done")
        rsum_done = sem("rsum_done")

        first, steady, after, last = -2, 2, BATCH - 2, BATCH + 1
        work = Uses([("V0", 1), ("V1", 1), ("V2", 1), ("O1", -1), ("V3", 1), ("K0", 2),
                     ("M1", 0), ("V4", 1), ("V5", 1), ("V6", 1), ("V7", 1), ("K1", 2),
                     ("V8", 1), ("O0", 0), ("V9", 1), ("V10", 1), ("V11", 1), ("M0", 1), ("K2", 2)], first, steady)
        AT = {(0, 0): "V0", (1, 0): "V1", (2, 0): "V2", (2, 1): "O1", (3, 0): "V3",
              (8, 0): "M1", (8, 1): "V4", (9, 0): "V5", (10, 0): "V6", (11, 0): "V7",
              (16, 0): "V8", (16, 1): "O0", (17, 0): "V9", (18, 0): "V10", (19, 0): "V11", (19, 1): "M0"}
        K_FROM = [4, 12, 20]
        CX_AHEAD = 2
        offset = dict(work.uses)

        def kbuf(par, u):
            return (UNITS * par + u) % 2

        def turns(j, par, u):
            return j * UNITS + (UNITS * par + u) // 2

        def step_units(t, s):
            return (0, MU - LEAD * PER + PER * s) if s < LEAD else (1, PER * (s - LEAD))

        block = ctx.enter_context(nc.Block())

        @block.sync
        def _(sp):
            sp.dma_start(wk[:, :, :], wkT.rearrange("(c p) n -> p c n", p=P)).then_inc(w_in, 16)

            def load_ctx(b, q):
                sp.dma_start(ctx_sb[:, q], ctxT[b].rearrange("(c p) k -> p c k", p=P)).then_inc(ctx_in[q], 16)

            def store_keys(t, u, p):
                sp.wait_ge(klo_done, (t + 2) * UNITS + u + 1)
                i = kbuf(p, u)
                sp.dma_start(kparts[t + 2].rearrange("r p k -> p r k")[:, :, u * UW:u * UW + UN[u]],
                             kp[:, i, :, 0:UN[u]]).then_inc(kp_sent[i], 16)

            def send_max(t, half, q):
                sp.wait_ge(w_read, work.count(t, f"M{half}"))
                for r in range(3):
                    sp.dma_start(qst[STACK + r:STACK + r + 1, q, HH * half:HH * half + HH, :],
                                 mrow[HH * r:HH * (r + 1), :]).then_inc(mrow_in, 16)

            def send_outputs(t, b, half):
                sp.wait_ge(w_read, work.count(t, f"O{half}"))
                sp.dma_start(o_out[b][:, half * 256:(half + 1) * 256],
                             otok[:, half * 256:(half + 1) * 256]).then_inc(o_sent[half], 16)

            for u in range(UNITS):
                sp.dma_start(ctx_sb[:, 0, :, u * UW:u * UW + UN[u]],
                             ctxT[0].rearrange("(c p) k -> p c k", p=P)[:, :, u * UW:u * UW + UN[u]]
                             ).then_inc(ctx_in[0] if u == UNITS - 1 else ctx_first[u], 16)
            sp.dma_start(wv[:, :, :], wvT.rearrange("(c p) n -> p c n", p=P)).then_inc(wv_in, 16)
            load_ctx(1, 1)

            def body(j, p):
                t = j * 2 + p
                mx, st = there(t + 1), there(t)
                q = 1 - p
                if mx:
                    if not isinstance(t, int) or t >= 1:
                        sp.wait_ge(st_full, STEPS * t)
                    sp.dma_start(qst[0:STACK, q].rearrange("p h n -> p (h n)"), qstack[t + 1]).then_inc(qst_in[q], 16)
                    b = j + (p + 1) // 2
                    for u in (1, 2):
                        sp.wait_ge(kp_sent[kbuf(q, u)], (turns(b, q, u) + 1) * 16)
                    for r, part in enumerate((0, 1, 2, 0, 1, 0)):
                        sp.dma_start(kst[HD * r:HD * (r + 1), q],
                                     kparts[t + 1][part].rearrange("(g d) k -> d g k", g=KV)).then_inc(kst_in[q], 16)
                if there(t - 1):
                    send_outputs(t, t - 1, 1)
                if there(t + 2):
                    store_keys(t, 0, p)
                if st:
                    send_max(t, 1, p)
                if there(t + 2):
                    store_keys(t, 1, p)
                if st:
                    send_outputs(t, t, 0)
                if mx:
                    send_max(t, 0, q)
                if there(t + 3) and (not isinstance(t, int) or t > first):
                    if there(t + 1):
                        sp.wait_ge(w_full, work.count(t, "V11"))
                    load_ctx(t + 3, q)
                if there(t + 2):
                    store_keys(t, 2, p)

            run_slots(sp, body, first, steady, BATCH - 4, last)
            for half in range(2):
                sp.wait_ge(o_sent[half], 16 * BATCH)
            for i in range(2):
                sp.wait_ge(kp_sent[i], 16 * (BATCH * UNITS // 2))

        @block.tensor
        def _(pe):
            pe.wait_ge(wk_split, 1)

            def body(j, p):
                t = j * 2 + p
                q = 1 - p

                def use(name):
                    wait_free(pe, w_read, work, t, name)

                if isinstance(t, int) and t == first + 1:
                    pe.wait_ge(const_done, 8)
                    pe.wait_ge(wv_in, 16)

                def piece(name):
                    if not there(t + offset[name]):
                        return
                    use(name)
                    kind, n = name[0], int(name[1:])
                    if kind == "V":
                        if n == 0:
                            pe.wait_ge(ctx_in[q], (j + (p + 1) // 2 + 1) * 16)
                        for c in range(CH):
                            done = nc.tensor.matmul(ps_w[0:KTN[n], 0:P], ctx_sb[:, q, c, n * KTW:n * KTW + KTN[n]],
                                                    wv[:, c, :], start=c == 0, stop=c == CH - 1)
                    elif kind == "O":
                        pe.wait_ge(pv_read, (t + offset[name]) * 2 + n + 1)
                        for r in range(REP):
                            done = nc.tensor.transpose(ps_w[0:SEQ, r * P:(r + 1) * P], oT[:, r * SEQ:(r + 1) * SEQ], ident[:, :])
                    else:
                        pe.wait_ge(mlo_done, (t + offset[name]) * 2 + n + 1)
                        done = nc.tensor.transpose(ps_w[:, 0:SEQ // 2].bitcast(BF16), mparts[:, :], identb[0:SEQ, 0:SEQ])
                    done.then_inc(w_full, 1)

                def keys(u, c):
                    if not there(t + 2):
                        return
                    if c == 0:
                        use(f"K{u}")
                    pe.wait_ge(cx_split, ((t + 2) * UNITS + u) * CH + c + 1)
                    out = ps_w[:, 0:UN[u]]
                    nc.tensor.matmul(out, wk_h[:, c, :], cx_h[:, c, 0:UN[u]], start=c == 0, stop=False)
                    nc.tensor.matmul(out, wk_l[:, c, :], cx_h[:, c, 0:UN[u]], start=False, stop=False)
                    done = nc.tensor.matmul(out, wk_h[:, c, :], cx_l[:, c, 0:UN[u]], start=False, stop=c == CH - 1)
                    done.then_inc(w_full if c == CH - 1 else cx_used, 1)

                def maxima(s, k):
                    d, unit = step_units(t, s)
                    if not there(t + d):
                        return
                    unit += k
                    par = (p + d) % 2
                    if unit == 0:
                        b = j + (p + 1) // 2
                        pe.wait_ge(qst_in[par], (b + 1) * 16)
                        pe.wait_ge(kst_in[par], (b + 1) * (TERMS * 16))
                    n = (t + d) * MU + unit - 1
                    if not isinstance(n, int) or n > 0:
                        pe.wait_ge(mx_read, n)
                    h, u = unit // UNITS, unit % UNITS
                    nc.tensor.matmul(ps_mx[0:SEQ, unit % 2, 0:UN[u]], qst[0:STACK, par, h, :],
                                     kst[0:STACK, par, h // REP, u * UW:u * UW + UN[u]], start=True, stop=True
                                     ).then_inc(mx_full, 1)

                def scores(s):
                    half, k = s // KT, s % KT
                    if k == 0:
                        pe.wait_ge(mrow_in, (t * 2 + half + 1) * 48)
                    if not isinstance(t, int) or t > 0 or s > 0:
                        pe.wait_ge(exp_done, t * STEPS + s)
                    for c in range(4):
                        done = nc.tensor.matmul(ps_st[0:KTN[k], c, 0:4 * SEQ],
                                                kst[0:AUG, p, 4 * half + c, k * KTW:k * KTW + KTN[k]],
                                                qst[0:AUG, p, 4 * (4 * half + c):4 * (4 * half + c) + 4, :].rearrange("p h n -> p (h n)"),
                                                start=True, stop=True)
                    done.then_inc(st_full, 1)

                def values(t, par, s, cs):
                    half, k = s // KT, s % KT
                    if cs[0] == 0:
                        pe.wait_ge(exp_done, t * STEPS + s + 1)
                        if k == 0:
                            n = t * 2 + half
                            if not isinstance(n, int) or n > 0:
                                pe.wait_ge(pv_read, n)
                            if half == 0:
                                pe.wait_ge(w_read, work.count(t - 1, "V11"))
                    for c in cs:
                        done = nc.tensor.matmul(ps_pv[VW * c:VW * (c + 1), 0:4 * SEQ],
                                                vaug[0:KTN[k], par, k, 4 * half + c, :], prob[0:KTN[k], s % 2, c, :],
                                                start=k == 0, stop=k == KT - 1)
                    if cs[-1] == 3:
                        done.then_inc(pv_done, 1)

                for s in range(STEPS):
                    if there(t):
                        scores(s)
                    maxima(s, 0)
                    for u in range(UNITS):
                        if K_FROM[u] <= s < K_FROM[u] + CH:
                            keys(u, s - K_FROM[u])
                    if (s, 0) in AT:
                        piece(AT[s, 0])
                    for n, cs in enumerate(((0, 1), (2, 3))):
                        maxima(s, 1 + n)
                        if s > 0 and there(t):
                            values(t, p, s - 1, cs)
                        elif s == 0 and there(t - 1):
                            values(t - 1, q, STEPS - 1, cs)
                    if (s, 1) in AT:
                        piece(AT[s, 1])
                    maxima(s, 3)

            run_slots(pe, body, first, steady, after, last)

        def cx_free(engine, t, u, c):
            b = t + 2
            n = b * UNITS + u
            if isinstance(n, int) and n == 0:
                return
            if c == CH - 1:
                engine.wait_ge(w_full, work.count(t, f"K{u - 1}") if u > 0 else work.count(t - 1, f"K{UNITS - 1}"))
            else:
                engine.wait_ge(cx_used, (n - 1) * (CH - 1) + c + 1)

        def cx_from(p, u, c):
            return ctx_sb[:, p, c, u * UW:u * UW + UN[u]]

        @block.scalar
        def _(act):
            act.wait_ge(w_in, 16)
            nc.scalar.copy(wk_h[:, :, :], wk[:, :, :]).then_inc(wk_high, 1)

            def body(j, p):
                t = j * 2 + p
                if isinstance(t, int) and t == first + 1:
                    act.wait_ge(const_done, 8)
                q = 1 - p

                def read_values(name):
                    n = int(name[1:])
                    act.wait_ge(w_full, work.count(t, name))
                    if n == 0 and there(t - 1):
                        act.wait_ge(pv_done, STEPS * t)
                    nc.scalar.copy(vaug[0:KTN[n], q, n, :, 0:HD],
                                   ps_w[0:KTN[n], 0:P].rearrange("p (g d) -> p g d", g=KV)).then_inc(w_read, 1)

                def split_ctx(u, c):
                    if isinstance(t, int) and t == first and u < UNITS - 1:
                        act.wait_ge(ctx_first[u], 16)
                    elif u == 0 or isinstance(t, int) and t == first:
                        act.wait_ge(ctx_in[p], (j + 2) * 16)
                    cx_free(act, t, u, c)
                    nc.scalar.copy(cx_h[:, c, 0:UN[u]], cx_from(p, u, c)).then_inc(cx_high, 1)

                for s in range(STEPS):
                    if there(t):
                        act.wait_ge(st_full, t * STEPS + s + 1)
                        n = t * STEPS + s - 1
                        if not isinstance(n, int) or n > 0:
                            act.wait_ge(pv_done, n)
                        nc.scalar.activation(prob[0:KTN[s % KT], s % 2], ps_st[0:KTN[s % KT], :, 0:4 * SEQ],
                                             ACT.Exp).then_inc(exp_done, 1)
                    if s == 0 and there(t - 1):
                        act.wait_ge(pv_done, STEPS * t)
                        nc.scalar.copy(oT[:, :], ps_pv[:, 0:4 * SEQ]).then_inc(pv_read, 1)
                    if s == KT and there(t):
                        act.wait_ge(pv_done, t * STEPS + KT)
                        nc.scalar.copy(oT[:, :], ps_pv[:, 0:4 * SEQ]).then_inc(pv_read, 1)
                    for m in range(2):
                        name = AT.get((s, m))
                        if name and name[0] == "V" and there(t + 1):
                            read_values(name)
                    for u in range(UNITS):
                        if 0 <= s + CX_AHEAD - K_FROM[u] < CH and there(t + 2):
                            split_ctx(u, s + CX_AHEAD - K_FROM[u])
                    for u in range(UNITS):
                        if s == K_FROM[u] + CH - 1 and there(t + 2):
                            act.wait_ge(w_full, work.count(t, f"K{u}"))
                            i = kbuf(p, u)
                            n = turns(j + 1, p, u)
                            if not isinstance(n, int) or n > 0:
                                act.wait_ge(kp_sent[i], n * 16)
                            nc.scalar.copy(kp[:, i, 0, 0:UN[u]], ps_w[:, 0:UN[u]]).then_inc(khi_done, 1)

            run_slots(act, body, first, steady, after, last)

        @block.vector
        def _(dve):
            dve.wait_ge(wk_high, 1)
            nc.vector.tensor_tensor(wk_l[:, :, :], wk[:, :, :], wk_h[:, :, :].bitcast(F32), ALU.subtract).then_inc(wk_split, 1)

            def body(j, p):
                t = j * 2 + p
                if isinstance(t, int) and t == first + 1:
                    dve.wait_ge(const_done, 8)
                q = 1 - p

                def outputs(b, half):
                    o = ps_w[0:SEQ, :].rearrange("p (r c v) -> p r c v", r=REP, c=4)
                    dve.wait_ge(w_full, work.count(t, f"O{half}"))
                    n = b * 2 + half
                    nc.vector.reciprocal(rsum[:, :].rearrange("p (r c) -> p r c", r=REP), o[:, :, :, HD]).then_inc(rsum_done, 1)
                    dve.wait_ge(rsum_done, n + 1)
                    if not isinstance(b, int) or b > 0:
                        dve.wait_ge(o_sent[half], b * 16)
                    nc.vector.tensor_tensor(
                        otok[:, half * 256:(half + 1) * 256].rearrange("p (c r d) -> p r c d", c=4, r=REP),
                        o[:, :, :, 0:HD],
                        rsum[:, :].rearrange("p (r c) -> p r c", r=REP).unsqueeze(3).to_broadcast([SEQ, REP, 4, HD]),
                        ALU.mult).then_inc(w_read, 1)

                def max_parts(b, half):
                    n = b * 2 + half + 1

                    def negated():
                        dve.wait_ge(mx_read, b * MU + (half + 1) * (MU // 2))
                        nc.vector.tensor_reduce(nmax[:, :], pmax[:, HH * half:HH * (half + 1), :], AX.X, ALU.max,
                                                negate=True).then_inc(nmax_done, 1)

                    def high():
                        dve.wait_ge(nmax_done, n)
                        nc.vector.tensor_copy(mpart[0], nmax[:, :]).then_inc(mhi_done, 1)

                    def rest():
                        dve.wait_ge(mhi_done, n)
                        nc.vector.tensor_tensor(nrest[:, :], nmax[:, :], mpart[0], ALU.subtract).then_inc(nrest_done, 1)

                    def mid():
                        dve.wait_ge(nrest_done, n)
                        nc.vector.tensor_copy(mpart[1], nrest[:, :]).then_inc(mmid_done, 1)

                    def low():
                        dve.wait_ge(mmid_done, n)
                        nc.vector.tensor_tensor(mpart[2], nrest[:, :], mpart[1], ALU.subtract).then_inc(mlo_done, 1)

                    return negated, high, rest, mid, low

                def max_rows(b, half):
                    n = b * 2 + half
                    dve.wait_ge(w_full, work.count(t, f"M{half}"))
                    if not isinstance(n, int) or n > 0:
                        dve.wait_ge(mrow_in, n * 48)
                    nc.vector.tensor_copy(mrow[:, :], ps_w[0:3 * HH, 0:SEQ // 2].bitcast(BF16)).then_inc(w_read, 1)

                def keys_rest(u):
                    n = (t + 2) * UNITS + u
                    dve.wait_ge(khi_done, n + 1)
                    if not isinstance(n, int) or n > 1:
                        dve.wait_ge(klo_done, n - 1)
                    nc.vector.tensor_tensor(kr[:, kbuf(p, u), 0:UN[u]], ps_w[:, 0:UN[u]], kp[:, kbuf(p, u), 0, 0:UN[u]],
                                            ALU.subtract).then_inc(w_read, 1)

                for s in range(STEPS):
                    d, unit0 = step_units(t, s)
                    for k in range(PER):
                        if there(t + d):
                            unit = unit0 + k
                            dve.wait_ge(mx_full, (t + d) * MU + unit + 1)
                            h, u = unit // UNITS, unit % UNITS
                            nc.vector.reduce_max(pmax[:, h, u:u + 1], ps_mx[0:SEQ, unit % 2, 0:UN[u]], AX.X).then_inc(mx_read, 1)
                        at = s * PER + k
                        if 0 <= at - LEAD * PER < 5 and there(t):
                            max_parts(t, 1)[at - LEAD * PER]()
                        if 0 <= at - (KT + LEAD) * PER < 5 and there(t + 1):
                            max_parts(t + 1, 0)[at - (KT + LEAD) * PER]()
                        if (s, k) == (8, 0) and there(t):
                            max_rows(t, 1)
                        if (s, k) == (19, 2) and there(t + 1):
                            max_rows(t + 1, 0)
                        if (s, k) == (2, 2) and there(t - 1):
                            outputs(t - 1, 1)
                        if (s, k) == (16, 2) and there(t):
                            outputs(t, 0)
                        for u in range(UNITS):
                            if (s, k) == (K_FROM[u] + CH - 1, 2) and there(t + 2):
                                keys_rest(u)

            run_slots(dve, body, first, steady, after, last)

        @block.gpsimd
        def _(pool):
            nc.gpsimd.memset(zero[:, :], 0.0).then_inc(const_done, 1)
            pool.wait_ge(const_done, 1)

            def constants():
                identity(nc, pool, ident[:, :], zeroed).then_inc(const_done, 1)
                nc.gpsimd.memset(identb[:, :], 0.0).then_inc(zeroed, 1)
                nc.gpsimd.memset(vaug[:, :, :, :, :], 0.0).then_inc(zeroed, 1)
                pool.wait_ge(zeroed, 3)
                nc.gpsimd.affine_select(out=identb[:, :], in_=identb[:, :], compare_op=ALU.not_equal, fill=1.0, base=0,
                                        pattern=[[-1, P]], channel_multiplier=1).then_inc(const_done, 1)
                nc.gpsimd.memset(mparts[:, 3 * HH:P], 0.0).then_inc(const_done, 1)
                for i in range(2):
                    pool.wait_ge(const_done, 2 * i + 4)
                    nc.gpsimd.memset(vaug[:, i, :, :, HD:HD + 1], 1.0).then_inc(const_done, 1)
                    pool.wait_ge(const_done, 2 * i + 5)
                    nc.gpsimd.memset(kst[STACK:P, i, :, :], 1.0).then_inc(const_done, 1)
                pool.wait_ge(const_done, 8)

            def body(j, p):
                t = j * 2 + p
                if isinstance(t, int) and t == first + 1:
                    constants()
                if not there(t + 2):
                    return
                for u in range(UNITS):
                    n = (t + 2) * UNITS + u + 1
                    i = kbuf(p, u)
                    for c in range(CH):
                        pool.wait_ge(cx_high, ((t + 2) * UNITS + u) * CH + c + 1)
                        nc.gpsimd.tensor_tensor(cx_l[:, c, 0:UN[u]], cx_from(p, u, c), cx_h[:, c, 0:UN[u]].bitcast(F32),
                                                ALU.subtract).then_inc(cx_split, 1)
                    pool.wait_ge(w_read, work.count(t, f"K{u}"))
                    nc.gpsimd.tensor_tensor(kp[:, i, 1, 0:UN[u]], kr[:, i, 0:UN[u]], zero[:, :].to_broadcast([P, UN[u]]),
                                            ALU.add).then_inc(kmid_done, 1)
                    pool.wait_ge(kmid_done, n)
                    nc.gpsimd.tensor_tensor(kp[:, i, 2, 0:UN[u]], kr[:, i, 0:UN[u]], kp[:, i, 1, 0:UN[u]],
                                            ALU.subtract).then_inc(klo_done, 1)

            run_slots(pool, body, first, steady, after, last)
def output_projection(nc, o_in, x1_in, woT, x2_out, x2T_out):
    with ExitStack() as ctx:
        def sb(name, shape, dt):
            return ctx.enter_context(nc.sbuf_tensor("o_" + name, shape, dt))

        def sem(name):
            return ctx.enter_context(nc.semaphore("o_" + name))

        PAIRS = BATCH // 2

        wo_f = sb("wo_f", [P, CH, HID], F32)
        wo_h = sb("wo_h", [P, CH, HID], F32R)
        wo_l = sb("wo_l", [P, CH, HID], F32R)
        ident = sb("ident", [P, P], F32)
        minus_half = sb("minus_half", [SEQ, 2], F32)
        eps = sb("eps", [SEQ, 2], F32)
        o_sb = sb("o_sb", [SEQ, 2, 2, HID], F32)
        x1 = sb("x1", [SEQ, 2, 2, HID], F32)
        oT_h = sb("oT_h", [P, 2, 2, CH, SEQ], F32R)
        oT_l = sb("oT_l", [P, 2, 2, CH, SEQ], F32R)
        res = sb("res", [SEQ, 2, 2, HID], F32)
        x2 = sb("x2", [SEQ, 2, 2, HID], F32)
        x2T = sb("x2T", [P, 2, CH, 2, SEQ], F32)
        stats = sb("stats", [SEQ, 2, 6], F32)
        mv = sb("mv", [SEQ, 2, 2], F32)
        ve = sb("ve", [SEQ, 2], F32)
        rstd = sb("rstd", [SEQ, 2, 2], F32)

        ps_t = ctx.enter_context(nc.psum_tensor("o_ps_t", [P, 2, 2, 512], F32))
        ps_o = ctx.enter_context(nc.psum_tensor("o_ps_o", [P, 2, 512], F32))
        ps_x = ctx.enter_context(nc.psum_tensor("o_ps_x", [P, 2, 512], F32))

        w_in = sem("w_in")
        w_high = sem("w_high")
        w_split = sem("w_split")
        zeroed = sem("zeroed")
        const_done = sem("const_done")
        o_load = [sem(f"o_load{i}") for i in range(2)]
        x1_load = [sem(f"x1_load{i}") for i in range(2)]
        x2_sent = [sem(f"x2_sent{i}") for i in range(2)]
        x2T_sent = [sem(f"x2T_sent{i}") for i in range(2)]
        oT_full = sem("oT_full")
        oT_high = sem("oT_high")
        oT_split = sem("oT_split")
        proj_full = sem("proj_full")
        res_done = sem("res_done")
        stats_done = sem("stats_done")
        mv_done = sem("mv_done")
        ve_done = sem("ve_done")
        rstd_done = sem("rstd_done")
        x2_done = sem("x2_done")
        x2T_full = sem("x2T_full")
        x2T_done = sem("x2T_done")

        def pairs(batches):
            return batches.rearrange("(t b) s n -> t s b n", b=2)

        def there(pair):
            return not isinstance(pair, int) or 0 <= pair < PAIRS

        def from_slot(t, n):
            return not isinstance(t, int) or t >= n

        first, steady, after, last = 0, 4, PAIRS, PAIRS + 2
        block = ctx.enter_context(nc.Block())

        @block.sync
        def _(sp):
            def load_o(t, p):
                sp.dma_start(o_sb[:, p], pairs(o_in)[t]).then_inc(o_load[p], 16)

            def load_x1(t, p):
                sp.dma_start(x1[:, p], pairs(x1_in)[t]).then_inc(x1_load[p], 16)

            load_o(0, 0)
            sp.dma_start(wo_f[:, :, :], woT.rearrange("(c p) n -> p c n", p=P)).then_inc(w_in, 16)
            load_o(1, 1)
            load_x1(0, 0)
            load_x1(1, 1)

            def body(j, p):
                t = j * 2 + p
                if there(t + 2):
                    sp.wait_ge(oT_full, t + 1)
                    load_o(t + 2, p)
                if there(t - 1) and there(t + 1):
                    sp.wait_ge(res_done, t)
                    load_x1(t + 1, 1 - p)
                if there(t - 2):
                    sp.wait_ge(x2_done, t - 1)
                    sp.dma_start(pairs(x2_out)[t - 2], x2[:, p]).then_inc(x2_sent[p], 16)
                    sp.wait_ge(x2T_done, t - 1)
                    sp.dma_start(x2T_out[j - 1][:, :, 2 * p:2 * p + 2], x2T[:, p]).then_inc(x2T_sent[p], 16)

            run_slots(sp, body, first, steady, PAIRS - 2, last)
            for i in range(2):
                sp.wait_ge(x2_sent[i], 16 * (PAIRS // 2))
                sp.wait_ge(x2T_sent[i], 16 * (PAIRS // 2))

        @block.tensor
        def _(pe):
            pe.wait_ge(const_done, 3)

            def body(j, p):
                t = j * 2 + p
                if there(t):
                    pe.wait_ge(o_load[p], (j + 1) * 16)
                    if from_slot(t, 2):
                        pe.wait_ge(oT_split, t - 1)
                    for b in range(2):
                        for c in range(CH):
                            done = nc.tensor.transpose(ps_t[:, p, b, c * SEQ:(c + 1) * SEQ],
                                                       o_sb[:, p, b, c * P:(c + 1) * P], ident[0:SEQ, 0:SEQ])
                    done.then_inc(oT_full, 1)
                if there(t - 1):
                    if isinstance(t, int) and t == 1:
                        pe.wait_ge(w_split, 1)
                    pe.wait_ge(oT_split, t)
                    if from_slot(t, 2):
                        pe.wait_ge(res_done, t - 1)
                    for b in range(2):
                        done = triple(nc, ps_o[0:SEQ, b, :],
                                      [(oT_h[:, 1 - p, b, c, :], oT_l[:, 1 - p, b, c, :]) for c in range(CH)],
                                      [(wo_h[:, c, :], wo_l[:, c, :]) for c in range(CH)])
                    done.then_inc(proj_full, 1)
                if there(t - 2):
                    pe.wait_ge(x2_done, t - 1)
                    if from_slot(t, 3):
                        pe.wait_ge(x2T_done, t - 2)
                    for b in range(2):
                        for c in range(CH):
                            done = nc.tensor.transpose(ps_x[:, b, c * SEQ:(c + 1) * SEQ],
                                                       x2[:, p, b, c * P:(c + 1) * P], ident[0:SEQ, 0:SEQ])
                    done.then_inc(x2T_full, 1)

            run_slots(pe, body, first, steady, after, last)

        @block.scalar
        def _(act):
            act.wait_ge(w_in, 16)
            nc.scalar.copy(wo_h[:, :, :], wo_f[:, :, :]).then_inc(w_high, 1)

            def body(j, p):
                t = j * 2 + p
                if there(t):
                    act.wait_ge(oT_full, t + 1)
                    if from_slot(t, 2):
                        act.wait_ge(proj_full, t - 1)
                    nc.scalar.copy(oT_h[:, p], ps_t[:, p, :, 0:CH * SEQ].rearrange("p b (c q) -> p b c q", c=CH)
                                   ).then_inc(oT_high, 1)
                if there(t - 2):
                    act.wait_ge(x2T_full, t - 1)
                    if from_slot(t, 4):
                        act.wait_ge(x2T_sent[p], (j - 1) * 16)
                    nc.scalar.copy(x2T[:, p], ps_x[:, :, 0:CH * SEQ].rearrange("p b (c q) -> p c b q", c=CH)
                                   ).then_inc(x2T_done, 1)

            run_slots(act, body, first, steady, after, last)

        @block.vector
        def _(dve):
            dve.wait_ge(w_high, 1)
            nc.vector.tensor_tensor(wo_l[:, :, :], wo_f[:, :, :], wo_h[:, :, :].bitcast(F32), ALU.subtract).then_inc(w_split, 1)

            def body(j, p):
                t = j * 2 + p
                if there(t):
                    dve.wait_ge(oT_high, t + 1)
                    if from_slot(t, 2):
                        dve.wait_ge(proj_full, t - 1)
                    nc.vector.tensor_tensor(oT_l[:, p], ps_t[:, p, :, 0:CH * SEQ].rearrange("p b (c q) -> p b c q", c=CH),
                                            oT_h[:, p].bitcast(F32), ALU.subtract).then_inc(oT_split, 1)
                if there(t - 2):
                    dve.wait_ge(rstd_done, t - 1)
                    if from_slot(t, 4):
                        dve.wait_ge(x2_sent[p], (j - 1) * 16)
                        dve.wait_ge(x2T_full, t - 3)
                    for b in range(2):
                        done = nc.vector.tensor_scalar(x2[:, p, b, :], res[:, p, b, :], mv[:, b, 0:1], rstd[:, p, b:b + 1],
                                                       ALU.subtract, ALU.mult)
                    done.then_inc(x2_done, 1)
                if there(t - 1):
                    q = 1 - p
                    dve.wait_ge(proj_full, t)
                    dve.wait_ge(x1_load[q], (j + p) * 16)
                    if from_slot(t, 3):
                        dve.wait_ge(x2_done, t - 2)
                    nc.vector.tensor_tensor(res[:, q], ps_o[0:SEQ], x1[:, q], ALU.add).then_inc(res_done, 1)
                    dve.wait_ge(res_done, t)
                    if from_slot(t, 2):
                        dve.wait_ge(mv_done, t - 1)
                    for b in range(2):
                        done = nc.vector.bn_stats(stats[:, b, :], res[:, q, b, :])
                    done.then_inc(stats_done, 1)
                    dve.wait_ge(w_split, 1)
                    dve.wait_ge(stats_done, t)
                    if from_slot(t, 2):
                        dve.wait_ge(x2_done, t - 1)
                    for b in range(2):
                        done = nc.vector.bn_aggr(mv[:, b, :], stats[:, b, :])
                    done.then_inc(mv_done, 1)

            run_slots(dve, body, first, steady, after, last)

        @block.gpsimd
        def _(pool):
            identity(nc, pool, ident[:, :], zeroed).then_inc(const_done, 1)
            nc.gpsimd.memset(minus_half[:, :], -0.5).then_inc(const_done, 1)
            nc.gpsimd.memset(eps[:, :], EPS).then_inc(const_done, 1)
            pool.wait_ge(const_done, 3)

            def body(j, p):
                t = j * 2 + p
                if there(t - 1):
                    pool.wait_ge(mv_done, t)
                    nc.gpsimd.tensor_tensor(ve[:, :], mv[:, :, 1], eps[:, :], ALU.add).then_inc(ve_done, 1)
                    pool.wait_ge(ve_done, t)
                    if from_slot(t, 3):
                        pool.wait_ge(x2_done, t - 2)
                    nc.gpsimd.tensor_tensor(rstd[:, 1 - p, :], ve[:, :], minus_half[:, :], ALU.pow).then_inc(rstd_done, 1)

            run_slots(pool, body, first, steady, after, last)


def feed_forward(nc, x2_in, x2T_in, gate_in, gscale, up_in, uscale, down_in, dscale, low_scratch, y_out):
    with ExitStack() as ctx:
        def sb(name, shape, dt):
            return ctx.enter_context(nc.sbuf_tensor("f_" + name, shape, dt))

        def sem(name):
            return ctx.enter_context(nc.semaphore("f_" + name))

        GB = 4
        GROUPS = BATCH // GB
        TOK = GB * SEQ
        TILES = FFN // P
        PIECES = 3

        gate_h = sb("gate_h", [P, TILES, CH, P], F32R)
        gate_l = sb("gate_l", [P, TILES, CH, P], F32R)
        up_h = sb("up_h", [P, TILES, CH, P], F32R)
        up_l = sb("up_l", [P, TILES, CH, P], F32R)
        down_h = sb("down_h", [P, TILES, HID], F32R)
        down_l = sb("down_l", [P, TILES, HID], F32R)
        gs = sb("gs", [P, TILES], F32)
        us = sb("us", [P, TILES], F32)
        ds = sb("ds", [SEQ, HID], F32)
        minus_half = sb("minus_half", [SEQ, 1], F32)
        eps = sb("eps", [SEQ, 1], F32)
        xT_f = sb("xT_f", [P, CH, TOK], F32)
        xT_h = sb("xT_h", [P, CH, TOK], F32R)
        xT_l = sb("xT_l", [P, CH, TOK], F32R)
        act_g = sb("act_g", [P, TOK], F32)
        hid = sb("hid", [P, TOK], F32)
        hid_h = sb("hid_h", [P, TOK], F32R)
        hid_l = sb("hid_l", [P, TOK], F32R)
        stats = sb("stats", [SEQ, 6], F32)
        mv = sb("mv", [SEQ, 2, 2], F32)
        ve = sb("ve", [SEQ, 1], F32)
        rstd = sb("rstd", [SEQ, 1], F32)

        low_sum = sb("low_sum", [P, TILES * PIECES], F32)
        low_col = sb("low_col", [P, 1], F32)
        low_any = sb("low_any", [1, 1], F32)
        low_flag = sb("low_flag", [1, 1], I32)
        low_row = ds[0:1, 0:P]

        stage = sb("stage", [P, 2 * PIECES * HID], I32)

        def staged(tile, piece):
            at = (tile % 2 * PIECES + piece) * HID
            return stage[:, at:at + HID]

        def y(i):
            return stage[0:SEQ, i * HID:(i + 1) * HID].bitcast(F32)

        def x2(i):
            return stage[0:SEQ, (GB + i % 2) * HID:(GB + i % 2 + 1) * HID].bitcast(F32)

        ps_g = ctx.enter_context(nc.psum_tensor("f_ps_g", [P, 2, 512], F32))
        ps_u = ctx.enter_context(nc.psum_tensor("f_ps_u", [P, 2, 512], F32))
        ps_y = ctx.enter_context(nc.psum_tensor("f_ps_y", [P, GB, 512], F32))

        scale_in = sem("scale_in")
        const_done = sem("const_done")
        w_in = [[sem(f"w_in{i}_{k}") for k in range(PIECES)] for i in range(2)]
        w_high = sem("w_high")
        w_split = sem("w_split")
        low_sum_done = sem("low_sum_done")
        low_col_done = sem("low_col_done")
        low_out = sem("low_out")
        low_in = sem("low_in")
        low_any_done = sem("low_any_done")
        low_flag_done = sem("low_flag_done")
        ds_in = sem("ds_in")
        xT_in = sem("xT_in")
        xT_high = sem("xT_high")
        xT_split = sem("xT_split")
        x2_load = [sem(f"x2_load{i}") for i in range(2)]
        g_full = sem("g_full")
        u_full = sem("u_full")
        g_act = sem("g_act")
        hid_done = sem("hid_done")
        hid_high = sem("hid_high")
        hid_split = sem("hid_split")
        down_done = sem("down_done")
        y_scaled = sem("y_scaled")
        y_added = sem("y_added")
        stats_done = sem("stats_done")
        mv_done = sem("mv_done")
        ve_done = sem("ve_done")
        rstd_done = sem("rstd_done")
        out_done = sem("out_done")
        out_sent = sem("out_sent")

        def later(g):
            return not isinstance(g, int) or g > 0

        def groups(engine, body, finish):
            body(0)
            body(1)
            with engine.Fori(2, GROUPS) as g:
                body(g)
            finish()

        STATS_AT = [2 + 2 * i for i in range(GB)]
        NORM_AT = [3 + 2 * i for i in range(GB)]

        block = ctx.enter_context(nc.Block())

        @block.sync
        def _(sp):
            def outputs(g):
                for i in range(GB):
                    sp.wait_ge(out_done, g * GB + i + 1)
                    sp.dma_start(y_out[g * GB + i], y(i)).then_inc(out_sent, 16)

            def residuals(g):
                for i in range(GB):
                    sp.wait_ge(y_scaled, g * GB + 1)
                    if i >= 2:
                        sp.wait_ge(y_added, g * GB + i - 1)
                    sp.dma_start(x2(i), x2_in[g * GB + i]).then_inc(x2_load[i % 2], 16)

            def body(g):
                if not later(g):
                    for tile in range(2):
                        load_weights(tile)
                        if tile == 0:
                            sp.dma_start(xT_f[:, :, :], x2T_in[g].rearrange("p c b s -> p c (b s)")).then_inc(xT_in, 16)
                            sp.dma_start(gs[:, :], gscale).then_inc(scale_in, 16)
                            sp.dma_start(us[:, :], uscale).then_inc(scale_in, 16)
                    for tile in range(2, TILES):
                        load_weights(tile)
                    sp.wait_ge(low_col_done, 1)
                    sp.dma_start(low_scratch, low_col[:, :]).then_inc(low_out, 16)
                    sp.wait_ge(low_out, 16)
                    sp.dma_start(low_row, low_scratch.rearrange("p one -> one p")).then_inc(low_in, 16)
                    sp.wait_ge(low_any_done, 1)
                    sp.dma_start(ds[:, :], dscale.partition_broadcast(SEQ)).then_inc(ds_in, 16)
                else:
                    sp.wait_ge(xT_split, g)
                    sp.dma_start(xT_f[:, :, :], x2T_in[g].rearrange("p c b s -> p c (b s)")).then_inc(xT_in, 16)
                    residuals(g - 1)
                    outputs(g - 1)

            def load_weights(tile):
                for piece, src in enumerate((gate_in, up_in, down_in)):
                    if tile >= 2:
                        sp.wait_ge(low_sum_done, (tile - 2) * PIECES + piece + 1)
                    sp.dma_start(staged(tile, piece), src[tile]).then_inc(w_in[tile % 2][piece], 16)

            def finish():
                residuals(GROUPS - 1)
                outputs(GROUPS - 1)

            groups(sp, body, finish)
            sp.wait_ge(out_sent, 16 * BATCH)

        @block.tensor
        def _(pe):
            def body(g, low=True):
                def weights(tile, piece):
                    if not later(g):
                        pe.wait_ge(w_split, tile * PIECES + piece + 1)

                def product(out, columns, rows):
                    if low:
                        return triple(nc, out, columns, rows)
                    for c, ((high, _low), (row_h, row_l)) in enumerate(zip(columns, rows)):
                        nc.tensor.matmul(out, high, row_h, start=c == 0, stop=False)
                        done = nc.tensor.matmul(out, high, row_l, start=False, stop=c == CH - 1)
                    return done

                def hidden(tile):
                    n = g * TILES + tile
                    i = tile % 2
                    if later(g) or tile >= 2:
                        pe.wait_ge(hid_done, n - 1)
                    rows = [(xT_h[:, c, :], xT_l[:, c, :]) for c in range(CH)]
                    weights(tile, 0)
                    product(ps_g[:, i, 0:TOK], [(gate_h[:, tile, c, :], gate_l[:, tile, c, :]) for c in range(CH)],
                            rows).then_inc(g_full, 1)
                    weights(tile, 1)
                    product(ps_u[:, i, 0:TOK], [(up_h[:, tile, c, :], up_l[:, tile, c, :]) for c in range(CH)],
                            rows).then_inc(u_full, 1)

                def outputs(tile):
                    weights(tile, 2)
                    pe.wait_ge(hid_split, g * TILES + tile + 1)
                    if tile == 0 and later(g):
                        pe.wait_ge(y_scaled, g * GB)
                    for n in range(GB):
                        q = slice(n * SEQ, (n + 1) * SEQ)
                        for a, b in ((hid_h, down_h), (hid_h, down_l), (hid_l, down_h)) if low else (
                                (hid_h, down_h), (hid_l, down_h)):
                            first = a is hid_h and b is down_h
                            done = nc.tensor.matmul(ps_y[0:SEQ, n, :], a[:, q], b[:, tile, :], start=tile == 0 and first,
                                                    stop=tile == TILES - 1 and a is hid_l)
                    done.then_inc(down_done, 1)

                pe.wait_ge(xT_split, g + 1)
                for tile in range(TILES + 1):
                    if tile < TILES:
                        hidden(tile)
                    if tile > 0:
                        outputs(tile - 1)

            body(0)
            pe.wait_ge(low_flag_done, 1)
            some_low = pe.value_load(low_flag[0:1, 0:1], min_val=0, max_val=1)
            with pe.If(some_low == 1):
                with pe.Fori(1, GROUPS) as g:
                    body(g)
            with pe.Else():
                with pe.Fori(1, GROUPS) as g:
                    body(g, low=False)

        @block.scalar
        def _(act):
            def convert(tile):
                for piece, high in enumerate((gate_h, up_h, down_h)):
                    act.wait_ge(w_in[tile % 2][piece], 16 * (tile // 2 + 1))
                    nc.scalar.copy(high[:, tile].rearrange("p c n -> p (c n)") if piece < 2 else high[:, tile],
                                   staged(tile, piece)).then_inc(w_high, 1)

            def square_low(tile):
                for piece, low in enumerate((gate_l, up_l, down_l)):
                    n = tile * PIECES + piece
                    act.wait_ge(w_split, n + 1)
                    nc.scalar.activation(staged(tile, piece).bitcast(F32),
                                         (low[:, tile].rearrange("p c n -> p (c n)") if piece < 2 else low[:, tile]).bitcast(F32),
                                         ACT.Square, accum_out=low_sum[:, n:n + 1]).then_inc(low_sum_done, 1)

            def body(g):
                if not later(g):
                    convert(0)
                    convert(1)
                    square_low(0)
                    square_low(1)
                    act.wait_ge(scale_in, 32)
                for tile in range(TILES):
                    n = g * TILES + tile
                    if not later(g) and tile + 2 < TILES:
                        convert(tile + 2)
                    act.wait_ge(g_full, n + 1)
                    if later(g) or tile > 0:
                        act.wait_ge(hid_done, n)
                    nc.scalar.activation(act_g[:, :], ps_g[:, tile % 2, 0:TOK], ACT.Silu, scale=gs[:, tile:tile + 1]
                                         ).then_inc(g_act, 1)
                    if not later(g) and tile + 2 < TILES:
                        square_low(tile + 2)

            groups(act, body, lambda: None)

        @block.vector
        def _(dve):
            def convert(tile):
                for piece, (high, low) in enumerate(((gate_h, gate_l), (up_h, up_l), (down_h, down_l))):
                    def flat(part):
                        return part[:, tile].rearrange("p c n -> p (c n)") if piece < 2 else part[:, tile]

                    dve.wait_ge(w_high, tile * PIECES + piece + 1)
                    nc.vector.tensor_tensor(flat(low), staged(tile, piece), flat(high).bitcast(F32), ALU.subtract
                                            ).then_inc(w_split, 1)

            def low_parts():
                dve.wait_ge(low_sum_done, TILES * PIECES)
                nc.vector.reduce_max(low_col[:, :], low_sum[:, :], AX.X).then_inc(low_col_done, 1)

            def low_parts_flag():
                dve.wait_ge(low_in, 16)
                nc.vector.reduce_max(low_any[:, :], low_row, AX.X).then_inc(low_any_done, 1)
                dve.wait_ge(low_any_done, 1)
                nc.vector.tensor_scalar(low_flag[:, :], low_any[:, :], 0.0, None, ALU.is_gt).then_inc(low_flag_done, 1)

            def drain(g):
                dve.wait_ge(ds_in, 16)
                dve.wait_ge(down_done, g * TILES + TILES)
                if later(g):
                    dve.wait_ge(out_sent, g * (GB * 16))
                for i in range(GB):
                    nc.vector.tensor_tensor(y(i), ps_y[0:SEQ, i, :], ds[:, :], ALU.mult).then_inc(y_scaled, 1)

            def statistics(g, i):
                b = g * GB + i
                dve.wait_ge(y_added, b + 1)
                if i > 0 or later(g):
                    dve.wait_ge(mv_done, b)
                nc.vector.bn_stats(stats[:, :], y(i)).then_inc(stats_done, 1)
                dve.wait_ge(scale_in, 32)
                dve.wait_ge(stats_done, b + 1)
                if i >= 2:
                    dve.wait_ge(out_done, b - 1)
                nc.vector.bn_aggr(mv[:, i % 2, :], stats[:, :]).then_inc(mv_done, 1)

            def norm(g, i):
                b = g * GB + i
                dve.wait_ge(rstd_done, b + 1)
                nc.vector.tensor_scalar(y(i), y(i), mv[:, i % 2, 0:1], rstd[:, :], ALU.subtract, ALU.mult).then_inc(out_done, 1)

            def body(g):
                if not later(g):
                    convert(0)
                dve.wait_ge(xT_in, g * 16 + 16)
                if later(g):
                    dve.wait_ge(u_full, g * TILES)
                nc.vector.tensor_copy(xT_h[:, :, :], xT_f[:, :, :]).then_inc(xT_high, 1)
                dve.wait_ge(xT_high, g + 1)
                nc.vector.tensor_tensor(xT_l[:, :, :], xT_f[:, :, :], xT_h[:, :, :].bitcast(F32), ALU.subtract).then_inc(xT_split, 1)
                if later(g):
                    drain(g - 1)
                else:
                    convert(1)
                for tile in range(TILES):
                    n = g * TILES + tile
                    if not later(g) and tile + 2 < TILES:
                        convert(tile + 2)
                    dve.wait_ge(u_full, n + 1)
                    dve.wait_ge(g_act, n + 1)
                    if later(g) or tile > 0:
                        dve.wait_ge(hid_split, n)
                    nc.vector.scalar_tensor_tensor(hid[:, :], ps_u[:, tile % 2, 0:TOK], us[:, tile:tile + 1], act_g[:, :],
                                                   ALU.mult, ALU.mult).then_inc(hid_done, 1)
                    dve.wait_ge(hid_done, n + 1)
                    if later(g) or tile > 0:
                        dve.wait_ge(down_done, n)
                    nc.vector.tensor_copy(hid_h[:, :], hid[:, :]).then_inc(hid_high, 1)
                    dve.wait_ge(hid_high, n + 1)
                    nc.vector.tensor_tensor(hid_l[:, :], hid[:, :], hid_h[:, :].bitcast(F32), ALU.subtract).then_inc(hid_split, 1)
                    if not later(g) and tile == TILES - 3:
                        low_parts()
                    if not later(g) and tile == TILES - 2:
                        low_parts_flag()
                    if later(g) and tile in STATS_AT:
                        statistics(g - 1, STATS_AT.index(tile))
                    if later(g) and tile in NORM_AT:
                        norm(g - 1, NORM_AT.index(tile))

            def finish():
                drain(GROUPS - 1)
                statistics(GROUPS - 1, 0)
                for i in range(GB):
                    if i + 1 < GB:
                        statistics(GROUPS - 1, i + 1)
                    norm(GROUPS - 1, i)

            groups(dve, body, finish)

        @block.gpsimd
        def _(pool):
            nc.gpsimd.memset(minus_half[:, :], -0.5).then_inc(const_done, 1)
            nc.gpsimd.memset(eps[:, :], EPS).then_inc(const_done, 1)
            pool.wait_ge(const_done, 2)

            def add(g, i):
                b = g * GB + i
                pool.wait_ge(y_scaled, b + 1)
                half = g * (GB // 2) * 16 + (i // 2 + 1) * 16
                pool.wait_ge(x2_load[i % 2], half)
                nc.gpsimd.tensor_tensor(y(i), y(i), x2(i), ALU.add).then_inc(y_added, 1)

            def deviation(g, i):
                b = g * GB + i
                pool.wait_ge(mv_done, b + 1)
                if i > 0 or later(g):
                    pool.wait_ge(rstd_done, b)
                nc.gpsimd.tensor_tensor(ve[:, :], mv[:, i % 2, 1:2], eps[:, :], ALU.add).then_inc(ve_done, 1)
                pool.wait_ge(ve_done, b + 1)
                if i > 0 or later(g):
                    pool.wait_ge(out_done, b)
                nc.gpsimd.tensor_tensor(rstd[:, :], ve[:, :], minus_half[:, :], ALU.pow).then_inc(rstd_done, 1)

            def group(g):
                for i in range(GB):
                    add(g, i)
                for i in range(GB):
                    deviation(g, i)

            group(0)
            with pool.Fori(1, GROUPS) as g:
                group(g)


def program(nc, x, xT, ctxT, wqkv, bqkv, wout, bout, wqT, wkT, wvT, woT, lnw, gate, gscale, up, uscale, down, dscale, y):
    def scratch(name, shape, dt):
        return nc.dram_tensor(name, shape, dt, kind="Internal").ap()

    x1 = scratch("x1_scratch", (BATCH, SEQ, HID), F32)
    x2 = scratch("x2_scratch", (BATCH, SEQ, HID), F32)
    x2T = scratch("x2T_scratch", (BATCH // 4, P, CH, 4, SEQ), F32)
    o = scratch("o_scratch", (BATCH, SEQ, HID), F32)
    qstack = scratch("qstack_scratch", (BATCH, STACK, HEADS * SEQ), BF16)
    kparts = scratch("kparts_scratch", (BATCH, 3, P, CTX), BF16)
    low = scratch("low_scratch", (P, 1), F32)
    self_attention(nc, x, xT, wqkv, bqkv, wout, bout, wqT, lnw, x1, qstack)
    cross_attention(nc, ctxT, wkT, wvT, qstack, kparts, o)
    output_projection(nc, o, x1, woT, x2, x2T)
    feed_forward(nc, x2, x2T, gate, gscale, up, uscale, down, dscale, low, y)


def kernel(**inputs):
    import numpy as np
    import concourse.bacc as bacc
    from concourse.bass_utils import run_bass_kernel_spmd

    a = {name: np.asarray(value) for name, value in inputs.items()}
    tiles = FFN // P
    laid = {
        "x": a["x"],
        "xT": a["x"].transpose(0, 2, 1),
        "ctxT": a["ctx_4096"].transpose(0, 2, 1),
        "wqkv": a["L0_attn_attn_qkvw"],
        "bqkv": a["L0_attn_attn_qkvb"],
        "wout": a["L0_attn_attn_ow"],
        "bout": a["L0_attn_attn_ob"],
        "wqT": a["L0_xattn_wq"].T,
        "wkT": a["L0_xattn_wk"].T,
        "wvT": a["L0_xattn_wv"].T,
        "woT": a["L0_xattn_wo"].T,
        "lnw": a["L0_xattn_ln_w"],
        "gate": a["L0_ffn_gate_wq"].reshape(tiles, P, CH, P).transpose(0, 3, 2, 1).reshape(tiles, P, HID),
        "gscale": a["L0_ffn_gate_scale"].reshape(tiles, P).T,
        "up": a["L0_ffn_up_wq"].reshape(tiles, P, CH, P).transpose(0, 3, 2, 1).reshape(tiles, P, HID),
        "uscale": a["L0_ffn_up_scale"].reshape(tiles, P).T,
        "down": a["L0_ffn_down_wq"].T.reshape(tiles, P, HID),
        "dscale": a["L0_ffn_down_scale"],
    }
    nc = bacc.Bacc("TRN2", target_bir_lowering=False, num_devices=1)
    arrays, args = {}, []
    for name, value in laid.items():
        arrays[name] = np.ascontiguousarray(value)
        args.append(nc.dram_tensor(name, arrays[name].shape, mybir.dt.from_np(arrays[name].dtype),
                                   kind="ExternalInput").ap())
    args.append(nc.dram_tensor("y", (BATCH, SEQ, HID), F32, kind="ExternalOutput").ap())
    program(nc, *args)
    return run_bass_kernel_spmd(nc, [arrays], core_ids=[0]).results[0]["y"]
```
